# Optimizing a Trainium2 kernel written in Bass

```python
import numpy as np
import jax
import jax.numpy as jnp

def _softmax(x, axis=-1):
    return jax.nn.softmax(x, axis=axis)

def _gelu(x):
    return jax.nn.gelu(x, approximate=True)

def _silu(x):
    return jax.nn.silu(x)

def _sigmoid(x):
    return jax.nn.sigmoid(x)

def _layernorm(x, axis=-1, eps=1e-05):
    m = jnp.mean(x, axis=axis, keepdims=True)
    v = jnp.var(x, axis=axis, keepdims=True)
    return (x - m) / jnp.sqrt(v + eps)

def _scatter_add(tgt, idx, src, axis=0):
    return tgt.at[idx].add(src)

def _segment_sum(src, seg, n):
    return jax.ops.segment_sum(src, seg, n)
kernel_name = 'mk_adj_seq_d4_adj_r2_f8db68'

def setup_inputs(seed: int=0):
    np.random.seed(seed)
    _w = jnp.asarray

    def _rec_inputs():
        import jax
        import jax.numpy as jnp
        _gk = jax.random.key(seed)
        x = 7.22e-05 + 1 * jax.random.normal(jax.random.fold_in(_gk, 1), (32, 256, 256), jnp.float32)
        _a = jax.random.bernoulli(jax.random.fold_in(_gk, 2), 0.0625, (32, 256, 256))
        _a = jnp.logical_or(_a, jnp.swapaxes(_a, -1, -2))
        _a = jnp.logical_or(_a, jnp.eye(256, dtype=bool))
        adj = _a.astype(jnp.int32)
        return (x, adj)
    x, adj = _rec_inputs()

    def _L0_gnn_setup():
        import jax, jax.numpy as jnp
        import numpy as np
        import math
        D = 256
        B, L = (8, 1024)
        EPS = 1e-05

        def layer_norm(y, gamma, beta):
            mu = jnp.mean(y, axis=-1, keepdims=True)
            var = jnp.mean(jnp.square(y - mu), axis=-1, keepdims=True)
            return (y - mu) * jax.lax.rsqrt(var + EPS) * gamma + beta
        key = jax.random.key(seed)
        ks = jax.random.split(key, 8)
        s = 1.0 / math.sqrt(D)
        x = jax.random.normal(ks[0], (B, L, D), dtype=jnp.float32)
        adj = jax.random.randint(ks[1], (B, L, L), 0, 2, dtype=jnp.int32)
        Wq = jax.random.normal(ks[2], (D, D), dtype=jnp.float32) * s
        Wk = jax.random.normal(ks[3], (D, D), dtype=jnp.float32) * s
        Wv = jax.random.normal(ks[4], (D, D), dtype=jnp.float32) * s
        Wo = jax.random.normal(ks[5], (D, D), dtype=jnp.float32) * s
        bo = jnp.zeros((D,), dtype=jnp.float32)
        gamma = jnp.ones((D,), dtype=jnp.float32)
        beta = jnp.zeros((D,), dtype=jnp.float32)
        return {'x': x, 'adj': adj, 'Wq': Wq, 'Wk': Wk, 'Wv': Wv, 'Wo': Wo, 'bo': bo, 'gamma': gamma, 'beta': beta}
    _L0_gnn_all = _L0_gnn_setup()
    _L0_gnn_in = {k: v for k, v in _L0_gnn_all.items() if k in ('Wq', 'Wk', 'Wv', 'Wo', 'bo', 'gamma', 'beta')}
    del _L0_gnn_all

    def _L1_gnn_setup():
        import jax, jax.numpy as jnp
        import numpy as np
        B, N, D, H = (4, 1024, 256, 8)
        HD = D // H
        EPS = 1e-05
        key = jax.random.key(seed)
        ks = jax.random.split(key, 12)
        x = jax.random.normal(ks[0], (B, N, D), dtype=jnp.float32)
        adj = jax.random.randint(ks[1], (B, N, N), 0, 2, dtype=jnp.int32)
        adj = jnp.maximum(adj, jnp.eye(N, dtype=jnp.int32)[None, :, :])
        s = 1.0 / np.sqrt(D)
        Wq = jax.random.uniform(ks[2], (D, D), jnp.float32, -s, s)
        bq = jnp.zeros((D,), jnp.float32)
        Wk = jax.random.uniform(ks[3], (D, D), jnp.float32, -s, s)
        bk = jnp.zeros((D,), jnp.float32)
        Wv = jax.random.uniform(ks[4], (D, D), jnp.float32, -s, s)
        bv = jnp.zeros((D,), jnp.float32)
        Wo = jax.random.uniform(ks[5], (D, D), jnp.float32, -s, s)
        bo = jnp.zeros((D,), jnp.float32)
        gamma = jnp.ones((D,), jnp.float32)
        beta = jnp.zeros((D,), jnp.float32)
        return {'x': x, 'adj': adj, 'Wq': Wq, 'bq': bq, 'Wk': Wk, 'bk': bk, 'Wv': Wv, 'bv': bv, 'Wo': Wo, 'bo': bo, 'gamma': gamma, 'beta': beta}
    _L1_gnn_all = _L1_gnn_setup()
    _L1_gnn_in = {k: v for k, v in _L1_gnn_all.items() if k in ('Wq', 'bq', 'Wk', 'bk', 'Wv', 'bv', 'Wo', 'bo', 'gamma', 'beta')}
    del _L1_gnn_all

    def _L2_gnn_setup():
        import jax, jax.numpy as jnp
        import numpy as np
        B, N, E, FF, L = (8, 1024, 256, 128, 2)
        LN_EPS = 1e-05
        SCALE = float(np.sqrt(FF))

        def layer_norm(x, g, b):
            m = jnp.mean(x, axis=-1, keepdims=True)
            v = jnp.mean(jnp.square(x - m), axis=-1, keepdims=True)
            return (x - m) * jax.lax.rsqrt(v + LN_EPS) * g + b
        key = jax.random.key(seed)
        ks = jax.random.split(key, 9)
        s = 0.02
        node_fts = jax.random.normal(ks[0], (B, N, E), jnp.float32)
        rel_edges = jax.random.randint(ks[1], (B, N, N), 0, 2, jnp.int32)
        Wq = jax.random.normal(ks[2], (L, FF, E), jnp.float32) * s
        bq = jnp.zeros((L, FF), jnp.float32)
        Wk = jax.random.normal(ks[3], (L, FF, E), jnp.float32) * s
        bk = jnp.zeros((L, FF), jnp.float32)
        Wc = jax.random.normal(ks[4], (L, E, E), jnp.float32) * s
        ln_g = jnp.ones((L, E), jnp.float32)
        ln_b = jnp.zeros((L, E), jnp.float32)
        return {'node_fts': node_fts, 'rel_edges': rel_edges, 'Wq': Wq, 'bq': bq, 'Wk': Wk, 'bk': bk, 'Wc': Wc, 'ln_g': ln_g, 'ln_b': ln_b}
    _L2_gnn_all = _L2_gnn_setup()
    _L2_gnn_in = {k: v for k, v in _L2_gnn_all.items() if k in ('Wq', 'bq', 'Wk', 'bk', 'Wc', 'ln_g', 'ln_b')}
    del _L2_gnn_all

    def _L3_gnn_setup():
        import jax, jax.numpy as jnp
        import numpy as np
        import math
        D = 256
        B, L = (8, 1024)
        EPS = 1e-05

        def layer_norm(y, gamma, beta):
            mu = jnp.mean(y, axis=-1, keepdims=True)
            var = jnp.mean(jnp.square(y - mu), axis=-1, keepdims=True)
            return (y - mu) * jax.lax.rsqrt(var + EPS) * gamma + beta
        key = jax.random.key(seed)
        ks = jax.random.split(key, 8)
        s = 1.0 / math.sqrt(D)
        x = jax.random.normal(ks[0], (B, L, D), dtype=jnp.float32)
        adj = jax.random.randint(ks[1], (B, L, L), 0, 2, dtype=jnp.int32)
        Wq = jax.random.normal(ks[2], (D, D), dtype=jnp.float32) * s
        Wk = jax.random.normal(ks[3], (D, D), dtype=jnp.float32) * s
        Wv = jax.random.normal(ks[4], (D, D), dtype=jnp.float32) * s
        Wo = jax.random.normal(ks[5], (D, D), dtype=jnp.float32) * s
        bo = jnp.zeros((D,), dtype=jnp.float32)
        gamma = jnp.ones((D,), dtype=jnp.float32)
        beta = jnp.zeros((D,), dtype=jnp.float32)
        return {'x': x, 'adj': adj, 'Wq': Wq, 'Wk': Wk, 'Wv': Wv, 'Wo': Wo, 'bo': bo, 'gamma': gamma, 'beta': beta}
    _L3_gnn_all = _L3_gnn_setup()
    _L3_gnn_in = {k: v for k, v in _L3_gnn_all.items() if k in ('Wq', 'Wk', 'Wv', 'Wo', 'bo', 'gamma', 'beta')}
    del _L3_gnn_all
    return {'x': x, 'adj': adj, 'L0_gnn_Wq': _L0_gnn_in['Wq'], 'L0_gnn_Wk': _L0_gnn_in['Wk'], 'L0_gnn_Wv': _L0_gnn_in['Wv'], 'L0_gnn_Wo': _L0_gnn_in['Wo'], 'L0_gnn_bo': _L0_gnn_in['bo'], 'L0_gnn_gamma': _L0_gnn_in['gamma'], 'L0_gnn_beta': _L0_gnn_in['beta'], 'L1_gnn_Wq': _L1_gnn_in['Wq'], 'L1_gnn_bq': _L1_gnn_in['bq'], 'L1_gnn_Wk': _L1_gnn_in['Wk'], 'L1_gnn_bk': _L1_gnn_in['bk'], 'L1_gnn_Wv': _L1_gnn_in['Wv'], 'L1_gnn_bv': _L1_gnn_in['bv'], 'L1_gnn_Wo': _L1_gnn_in['Wo'], 'L1_gnn_bo': _L1_gnn_in['bo'], 'L1_gnn_gamma': _L1_gnn_in['gamma'], 'L1_gnn_beta': _L1_gnn_in['beta'], 'L2_gnn_Wq': _L2_gnn_in['Wq'], 'L2_gnn_bq': _L2_gnn_in['bq'], 'L2_gnn_Wk': _L2_gnn_in['Wk'], 'L2_gnn_bk': _L2_gnn_in['bk'], 'L2_gnn_Wc': _L2_gnn_in['Wc'], 'L2_gnn_ln_g': _L2_gnn_in['ln_g'], 'L2_gnn_ln_b': _L2_gnn_in['ln_b'], 'L3_gnn_Wq': _L3_gnn_in['Wq'], 'L3_gnn_Wk': _L3_gnn_in['Wk'], 'L3_gnn_Wv': _L3_gnn_in['Wv'], 'L3_gnn_Wo': _L3_gnn_in['Wo'], 'L3_gnn_bo': _L3_gnn_in['bo'], 'L3_gnn_gamma': _L3_gnn_in['gamma'], 'L3_gnn_beta': _L3_gnn_in['beta']}

def reference(x, adj, L0_gnn_Wq, L0_gnn_Wk, L0_gnn_Wv, L0_gnn_Wo, L0_gnn_bo, L0_gnn_gamma, L0_gnn_beta, L1_gnn_Wq, L1_gnn_bq, L1_gnn_Wk, L1_gnn_bk, L1_gnn_Wv, L1_gnn_bv, L1_gnn_Wo, L1_gnn_bo, L1_gnn_gamma, L1_gnn_beta, L2_gnn_Wq, L2_gnn_bq, L2_gnn_Wk, L2_gnn_bk, L2_gnn_Wc, L2_gnn_ln_g, L2_gnn_ln_b, L3_gnn_Wq, L3_gnn_Wk, L3_gnn_Wv, L3_gnn_Wo, L3_gnn_bo, L3_gnn_gamma, L3_gnn_beta):
    import jax
    import jax.numpy as jnp

    def _L0_gnn_ref(x, adj, Wq, Wk, Wv, Wo, bo, gamma, beta):
        import jax, jax.numpy as jnp
        import numpy as np
        import math
        D = 256
        B, L = (8, 1024)
        EPS = 1e-05

        def layer_norm(y, gamma, beta):
            mu = jnp.mean(y, axis=-1, keepdims=True)
            var = jnp.mean(jnp.square(y - mu), axis=-1, keepdims=True)
            return (y - mu) * jax.lax.rsqrt(var + EPS) * gamma + beta
        d_out = Wq.shape[1]
        scale = 1.0 / math.sqrt(d_out)
        Q = x @ Wq
        K = x @ Wk
        V = x @ Wv
        sc = jnp.einsum('bld,bmd->blm', Q, K) * scale
        mask = adj == 0
        sc = jnp.where(mask, -jnp.inf, sc)
        all_inf = jnp.all(mask, axis=-1, keepdims=True)
        sc = jnp.where(all_inf, 0.0, sc)
        w = jax.nn.softmax(sc, axis=-1)
        out = jnp.einsum('blm,bmd->bld', w, V)
        y = x + out @ Wo + bo
        return layer_norm(y, gamma, beta)

    def _L1_gnn_ref(x, adj, Wq, bq, Wk, bk, Wv, bv, Wo, bo, gamma, beta):
        import jax, jax.numpy as jnp
        import numpy as np
        B, N, D, H = (4, 1024, 256, 8)
        HD = D // H
        EPS = 1e-05
        b, n, d = x.shape
        scale = 1.0 / np.sqrt(HD).astype(np.float32)
        q = (x @ Wq + bq).reshape(b, n, H, HD)
        k = (x @ Wk + bk).reshape(b, n, H, HD)
        v = (x @ Wv + bv).reshape(b, n, H, HD)
        scores = jnp.einsum('bnhd,bmhd->bhnm', q, k) * scale
        mask = (adj == 0)[:, None, :, :]
        scores = jnp.where(mask, jnp.float32(-jnp.inf), scores)
        attn = jax.nn.softmax(scores, axis=-1)
        h = jnp.einsum('bhnm,bmhd->bnhd', attn, v).reshape(b, n, d)
        h = h @ Wo + bo
        y = h + x
        mu = jnp.mean(y, axis=-1, keepdims=True)
        var = jnp.mean(jnp.square(y - mu), axis=-1, keepdims=True)
        return (y - mu) * jax.lax.rsqrt(var + EPS) * gamma + beta

    def _L2_gnn_ref(node_fts, rel_edges, Wq, bq, Wk, bk, Wc, ln_g, ln_b):
        import jax, jax.numpy as jnp
        import numpy as np
        B, N, E, FF, L = (8, 1024, 256, 128, 2)
        LN_EPS = 1e-05
        SCALE = float(np.sqrt(FF))

        def layer_norm(x, g, b):
            m = jnp.mean(x, axis=-1, keepdims=True)
            v = jnp.mean(jnp.square(x - m), axis=-1, keepdims=True)
            return (x - m) * jax.lax.rsqrt(v + LN_EPS) * g + b
        x = node_fts
        mask = rel_edges == 0
        for k in range(L):
            q = jnp.einsum('bnd,fd->bnf', x, Wq[k]) + bq[k]
            kk = jnp.einsum('bnd,fd->bnf', x, Wk[k]) + bk[k]
            scores = jnp.einsum('bof,bif->boi', q, kk) / SCALE
            scores = jnp.where(mask, -10000000000.0, scores)
            attn = jax.nn.softmax(scores, axis=2)
            attn = jnp.where(mask, 0.0, attn)
            ctx = jnp.einsum('boi,bid->bod', attn, x)
            ctx = jnp.einsum('bnd,ed->bne', ctx, Wc[k])
            x = layer_norm(x + ctx, ln_g[k], ln_b[k])
        return x

    def _L3_gnn_ref(x, adj, Wq, Wk, Wv, Wo, bo, gamma, beta):
        import jax, jax.numpy as jnp
        import numpy as np
        import math
        D = 256
        B, L = (8, 1024)
        EPS = 1e-05

        def layer_norm(y, gamma, beta):
            mu = jnp.mean(y, axis=-1, keepdims=True)
            var = jnp.mean(jnp.square(y - mu), axis=-1, keepdims=True)
            return (y - mu) * jax.lax.rsqrt(var + EPS) * gamma + beta
        d_out = Wq.shape[1]
        scale = 1.0 / math.sqrt(d_out)
        Q = x @ Wq
        K = x @ Wk
        V = x @ Wv
        sc = jnp.einsum('bld,bmd->blm', Q, K) * scale
        mask = adj == 0
        sc = jnp.where(mask, -jnp.inf, sc)
        all_inf = jnp.all(mask, axis=-1, keepdims=True)
        sc = jnp.where(all_inf, 0.0, sc)
        w = jax.nn.softmax(sc, axis=-1)
        out = jnp.einsum('blm,bmd->bld', w, V)
        y = x + out @ Wo + bo
        return layer_norm(y, gamma, beta)
    x = _L0_gnn_ref(x, adj, L0_gnn_Wq, L0_gnn_Wk, L0_gnn_Wv, L0_gnn_Wo, L0_gnn_bo, L0_gnn_gamma, L0_gnn_beta)
    x = _L1_gnn_ref(x, adj, L1_gnn_Wq, L1_gnn_bq, L1_gnn_Wk, L1_gnn_bk, L1_gnn_Wv, L1_gnn_bv, L1_gnn_Wo, L1_gnn_bo, L1_gnn_gamma, L1_gnn_beta)
    x = _L2_gnn_ref(x, adj, L2_gnn_Wq, L2_gnn_bq, L2_gnn_Wk, L2_gnn_bk, L2_gnn_Wc, L2_gnn_ln_g, L2_gnn_ln_b)
    x = _L3_gnn_ref(x, adj, L3_gnn_Wq, L3_gnn_Wk, L3_gnn_Wv, L3_gnn_Wo, L3_gnn_bo, L3_gnn_gamma, L3_gnn_beta)
    return x

_drawn_inputs = setup_inputs


def setup_inputs(seed=0):
    import zlib

    import numpy as np

    out = dict(_drawn_inputs(seed))
    spreads = {'L0_gnn_bo': (0.0, 0.1),
     'L0_gnn_gamma': (1.0, 0.2),
     'L0_gnn_beta': (0.0, 0.1),
     'L1_gnn_bq': (0.0, 0.8),
     'L1_gnn_bk': (0.0, 0.8),
     'L1_gnn_bv': (0.0, 0.1),
     'L1_gnn_bo': (0.0, 0.1),
     'L1_gnn_gamma': (1.0, 0.2),
     'L1_gnn_beta': (0.0, 0.1),
     'L2_gnn_bq': (0.0, 0.8),
     'L2_gnn_bk': (0.0, 0.8),
     'L2_gnn_ln_g': (1.0, 0.2),
     'L2_gnn_ln_b': (0.0, 0.1),
     'L3_gnn_bo': (0.0, 0.1),
     'L3_gnn_gamma': (1.0, 0.2),
     'L3_gnn_beta': (0.0, 0.1)}
    factors = {'L1_gnn_Wq': 2.803, 'L1_gnn_Wk': 2.755, 'L2_gnn_Wq': 6.323, 'L2_gnn_Wk': 6.026}
    for name, (base, spread) in spreads.items():
        noise = np.random.default_rng([zlib.crc32(name.encode()), seed]).standard_normal(out[name].shape)
        drawn = base * np.exp(spread * noise) if base else spread * noise
        out[name] = jnp.asarray(drawn.astype(out[name].dtype))
    for name, factor in factors.items():
        out[name] = (out[name] * factor).astype(out[name].dtype)
    return out
```

```python
from contextlib import ExitStack

import concourse.bass as bass
from concourse import mybir

P = 128
N = 256
D = 256
C = N // P
HEADS = 8
HD = D // HEADS
LAYERS = 5
ONE_HEAD = [0, 2, 3, 4]
SLOTS = 2
FIRST = 1
BIG = 1.0e30
EPS = 1e-5

F32 = mybir.dt.float32
F32R = mybir.dt.float32r
F16 = mybir.dt.float16
BF16 = mybir.dt.bfloat16
I32 = mybir.dt.int32
ALU = mybir.AluOpType
ACT = mybir.ActivationFunctionType
AX = mybir.AxisListType

RAW = ["q0T", "k0T", "v0T", "o0", "q3T", "k3T", "v3T", "o3", "q1", "k1", "v1", "o1", "qk2", "qk3", "c2", "c3"]
USED = ["qk_0", "vo_0", "q1", "k1", "v1", "o1", "qk2", "c2", "qk3", "c3", "qk_4", "vo_4"]
ROWS = ["g0", "g1", "g2", "g3", "g4", "b0", "b1", "b2", "b3", "b4", "bo0", "bo1", "bo4"]
COLS = ["g0", "g1", "g2", "g3", "b0", "b1", "b2", "b3", "bq1", "bk1", "bv1", "bqk2", "bqk3"]

PROJ = {(0, "g"): 1, (0, "v"): 2, (1, "q"): 3, (1, "k"): 4, (1, "v"): 5, (2, "g"): 6, (2, "v"): 7,
        (3, "g"): 8, (3, "v"): 9, (4, "g"): 10, (4, "v"): 11}
PROJS = len(PROJ)
SCORE = {0: 1, 2: 10, 3: 11, 4: 12}
SCORES = 12
STACK_DMAS = 2 * 4 * 4


def graph_stack_kernel(nc, x, adj, weights, rows, cols, out):
    graphs = x.shape[0]
    turns = graphs // SLOTS
    with ExitStack() as ctx:
        def sb(name, shape, dt=F32):
            return ctx.enter_context(nc.sbuf_tensor(name, [P] + shape, dt))

        def sem(name):
            return ctx.enter_context(nc.semaphore(name))

        def sems(name):
            return [sem(f"{name}{s}") for s in range(SLOTS)]

        ident = sb("ident", [P])
        identb = sb("identb", [P], BF16)
        hi_w = {n: sb(f"wh_{n}", [C, D], F32R) for n in USED}
        lo_w = {n: sb(f"wl_{n}", [C, D], F32R) for n in USED}
        row = {n: sb(f"row_{n}", [D]) for n in ROWS}
        col = sb("col", [len(COLS), C])
        unit = sb("unit", [2, C])
        half = sb("half", [C])
        eps = sb("eps", [C])
        wait_cell = [sb(f"wait_cell{s}", [1]) for s in range(SLOTS)]
        stage = sb("stage", [4, C, D])
        spread = sb("spread", [C, P])

        def per_slot(name, shape, dt=F32):
            return [sb(f"{name}{s}", shape, dt) for s in range(SLOTS)]

        xin = per_slot("xin", [C, D])
        adj_sb = per_slot("adj_sb", [C, N], I32)
        mask = per_slot("mask", [C, N], BF16)
        xres = per_slot("xres", [C, D])
        xt = per_slot("xt", [C, N])
        xt_hi = per_slot("xt_hi", [C, N], F32R)
        xt_lo = per_slot("xt_lo", [C, N], F32R)
        g_hi = per_slot("g_hi", [C, N], F32R)
        g_lo = per_slot("g_lo", [C, N], F32R)
        v_hi = per_slot("v_hi", [C, D], F32R)
        v_lo = per_slot("v_lo", [C, D], F32R)
        prob = per_slot("prob", [C, N])
        pt_hi = per_slot("pt_hi", [C, N], F32R)
        pt_lo = per_slot("pt_lo", [C, N], F32R)
        k_hi, k_lo = pt_hi, pt_lo
        q_stack = per_slot("q_stack", [HEADS, N], F32R)
        k_stack = per_slot("k_stack", [HEADS, N], F32R)
        v_rest = prob
        v_parts = per_slot("v_parts", [C, HEADS, 3, HD + 1], BF16)
        shifted = per_slot("shifted", [2, C, N], BF16)
        ht_hi = per_slot("ht_hi", [2, C, N], F16)
        ht_lo = per_slot("ht_lo", [2, C, N], F16)
        ht = per_slot("ht", [2, C, N])
        head_out = per_slot("head_out", [C, HEADS, HD + 1])
        heads_n = per_slot("heads_n", [C, D])
        neg_max = per_slot("neg_max", [SCORES, C])
        alive = per_slot("alive", [C, HEADS])
        alive1 = per_slot("alive1", [C])
        total = per_slot("total", [C])
        scale_row = per_slot("scale_row", [C])
        scale_row2 = per_slot("scale_row2", [C])
        den = per_slot("den", [C, HEADS])
        inv = per_slot("inv", [C, HEADS])
        y = per_slot("y", [C, D])
        stats = per_slot("stats", [C, 6])
        mean_var = per_slot("mean_var", [C, 2])
        var_eps = per_slot("var_eps", [C])
        rstd = per_slot("rstd", [C])
        result = per_slot("result", [C, D])

        bank = [[ctx.enter_context(nc.psum_tensor(f"bank{s}{b}", [P, 512], F32)) for b in range(4)]
                for s in range(SLOTS)]

        def two(b):
            return b[:, :].rearrange("p (c n) -> p c n", c=C)

        cols_in, rows_in, ident_made = sem("cols_in"), sem("rows_in"), sem("ident_made")
        raw_in = [sem(f"raw_in{k}") for k in range(4)]
        raw_split, prep_product, prep_hi = sem("raw_split"), sem("prep_product"), sem("prep_hi")
        prep_chain, weights_ready = sem("prep_chain"), sem("weights_ready")
        const_made, rows_ready, spread_made, bias_product = sem("const_made"), sem("rows_ready"), sem("spread_made"), sem("bias_product")
        x_in, x_used = sems("x_in"), sems("x_used")
        adj_in, mask_made = sems("adj_in"), sems("mask_made")
        x_turned, xt_made, xt_hi_made, xt_lo_made = sems("x_turned"), sems("xt_made"), sems("xt_hi_made"), sems("xt_lo_made")
        projected, proj_hi, proj_lo = sems("projected"), sems("proj_hi"), sems("proj_lo")
        scored, max_found, exp_made = sems("scored"), sems("max_found"), sems("exp_made")
        p_turned, p_hi, p_lo = sems("p_turned"), sems("p_hi"), sems("p_lo")
        attended, summed, stats_made, mean_made = sems("attended"), sems("summed"), sems("stats_made"), sems("mean_made")
        inv_step = sems("inv_step")
        eps_added, rstd_made, normed, scaled_up, res_made = sems("eps_added"), sems("rstd_made"), sems("normed"), sems("scaled_up"), sems("res_made")
        q_stacked, k_stacked, v2_made, v3_made = sems("q_stacked"), sems("k_stacked"), sems("v2_made"), sems("v3_made")
        shift_made, scored_t, head_exp, head_lo = sems("shift_made"), sems("scored_t"), sems("head_exp"), sems("head_lo")
        head_done, head_read, heads_normed = sems("head_done"), sems("head_read"), sems("heads_normed")
        stored, heads_chain = sems("stored"), sems("heads_chain")

        block = ctx.enter_context(nc.Block())

        def cc(name, c):
            i = COLS.index(name)
            return col[:, i, c:c + 1]

        @block.sync
        def _(sp):
            for s in range(SLOTS):
                sp.sem_inc(stored[s], 16)
            sp.dma_start(col[:, :, :], cols).then_inc(cols_in, 16)
            for n, name in enumerate(RAW):
                if n >= 4:
                    sp.wait_ge(raw_split, n - 3)
                sp.dma_start(stage[:, n % 4], weights[n].rearrange("(c p) n -> p c n", p=P)).then_inc(raw_in[n % 4], 16)
                if n == 0:
                    for m, r in enumerate(ROWS):
                        sp.dma_start(row[r][:, :], rows[:, m, :]).then_inc(rows_in, 16)
            with sp.Fori(0, turns) as i:
                for s in range(SLOTS):
                    sp.wait_ge(x_used[s], FIRST + i)
                    sp.dma_start(xin[s][:, :, :], x[i * SLOTS + s].rearrange("(c p) d -> p c d", p=P)).then_inc(x_in[s], 16)
                    sp.wait_ge(mask_made[s], FIRST + i)
                    sp.dma_start(adj_sb[s][:, :, :], adj[i * SLOTS + s].rearrange("(c p) d -> p c d", p=P)).then_inc(adj_in[s], 16)
                for s in range(SLOTS):
                    for which, sources, dest, done, index in (
                            ("q", (g_hi, g_hi, g_lo, g_lo), q_stack, q_stacked, PROJ[1, "q"]),
                            ("k", (k_hi, k_lo, k_hi, k_lo), k_stack, k_stacked, PROJ[1, "k"])):
                        sp.wait_ge(proj_lo[s], FIRST + i * PROJS + index)
                        for part in range(4):
                            for h in range(4):
                                sp.dma_start(dest[s][32 * part:32 * part + 32, h::4, :].bitcast(F32),
                                             sources[part][s][32 * h:32 * h + 32, :, :].bitcast(F32)).then_inc(done[s], 16)
                for s in range(SLOTS):
                    sp.wait_ge(res_made[s], (i + 1) * (LAYERS + 1))
                    sp.dma_start(out[i * SLOTS + s].rearrange("(c p) d -> p c d", p=P), result[s][:, :, :]).then_inc(stored[s], 16)
            for s in range(SLOTS):
                sp.wait_ge(stored[s], 16 * (turns + 1))

        @block.tensor
        def _(pe):
            for s in range(SLOTS):
                pe.sem_inc(scored[s], FIRST)
            pe.wait_ge(ident_made, 3)
            for m in range(4):
                a, b = (2 * m) % 4, (2 * m + 1) % 4
                pe.wait_ge(raw_in[a], 16 * (m // 2 + 1))
                pe.wait_ge(raw_in[b], 16 * (m // 2 + 1))
                if m:
                    pe.wait_ge(prep_chain, m)
                for c in range(C):
                    for e in range(C):
                        mm = pe.matmul(two(bank[0][0])[:, c, :], stage[:, a, e, c * P:(c + 1) * P], stage[:, b, e, :],
                                       start=(e == 0), stop=(e == C - 1))
                mm.then_inc(prep_product, 1)
            pe.wait_ge(spread_made, 2)
            pe.wait_ge(raw_in[RAW.index("o1") % 4], 16 * (RAW.index("o1") // 4 + 1))
            for e in range(C):
                mm = pe.matmul(bank[0][1][:, 0:D], spread[:, e, :], stage[:, RAW.index("o1") % 4, e, :],
                               start=(e == 0), stop=(e == C - 1))
            mm.then_inc(bias_product, 1)
            pe.wait_ge(weights_ready, 1)
            pe.wait_ge(rows_ready, 1)

            def three(dst, l_hi, l_lo, r_hi, r_lo, first, last):
                pe.matmul(dst, l_hi, r_hi, start=first, stop=False)
                pe.matmul(dst, l_hi, r_lo, start=False, stop=False)
                return pe.matmul(dst, l_lo, r_hi, start=False, stop=last)

            def turn_x(i, s, l):
                dst = two(bank[s][0])
                if l == 0:
                    pe.wait_ge(x_in[s], (i + 1) * 16)
                    pe.wait_ge(p_lo[s], FIRST + i * LAYERS)
                else:
                    pe.wait_ge(normed[s], i * LAYERS + l)
                src = xin[s] if l == 0 else y[s]
                for c in range(C):
                    for d in range(C):
                        mm = pe.transpose(dst[:, d, c * P:(c + 1) * P], src[:, c, d * P:(d + 1) * P], ident[:, :])
                mm.then_inc(x_turned[s], 1)

            def project(i, s, l, what, b, weight, columns=D):
                dst = two(bank[s][b])
                h, w = hi_w[weight], lo_w[weight]
                for c in range(C):
                    for d in range(C):
                        k = slice(c * P, (c + 1) * P)
                        mm = three(dst[:, c, :], h[:, d, k], w[:, d, k], xt_hi[s][:, d, :], xt_lo[s][:, d, :],
                                   d == 0, d == C - 1)
                mm.then_inc(projected[s], 1)

            def values(i, s, l, b, weight):
                dst = two(bank[s][b])
                for c in range(C):
                    for d in range(C):
                        k = slice(c * P, (c + 1) * P)
                        mm = three(dst[:, c, :], xt_hi[s][:, d, k], xt_lo[s][:, d, k], hi_w[weight][:, d, :],
                                   lo_w[weight][:, d, :], d == 0, d == C - 1)
                mm.then_inc(projected[s], 1)

            def begin(i, s, l):
                pe.wait_ge(xt_hi_made[s], i * LAYERS + l + 1)
                pe.wait_ge(xt_lo_made[s], i * LAYERS + l + 1)
                if l == 0:
                    pe.wait_ge(summed[s], FIRST + i * LAYERS)
                    pe.wait_ge(proj_lo[s], FIRST + i * PROJS)
                    pe.wait_ge(exp_made[s], FIRST + i * len(ONE_HEAD))

            def g_and_v(i, s, l):
                begin(i, s, l)
                project(i, s, l, "g", 1, {0: "qk_0", 2: "qk2", 3: "qk3", 4: "qk_4"}[l])
                values(i, s, l, 2, {0: "vo_0", 2: "c2", 3: "c3", 4: "vo_4"}[l])

            def scores(i, s, l):
                dst = two(bank[s][3])
                pe.wait_ge(proj_lo[s], FIRST + i * PROJS + PROJ[l, "g"])
                if l == 0:
                    pe.wait_ge(mask_made[s], FIRST + i + 1)
                for c in range(C):
                    k = slice(c * P, (c + 1) * P)
                    pe.matmul(dst[:, c, :], identb[:, :], mask[s][:, c, :], start=True, stop=False)
                    if l in (0, 4):
                        for e in range(C):
                            mm = three(dst[:, c, :], g_hi[s][:, e, k], g_lo[s][:, e, k], xt_hi[s][:, e, :],
                                       xt_lo[s][:, e, :], False, e == C - 1)
                    else:
                        mm = three(dst[:, c, :], g_hi[s][:, 0, k], g_lo[s][:, 0, k], g_hi[s][:, 1, :],
                                   g_lo[s][:, 1, :], False, True)
                mm.then_inc(scored[s], 1)

            def turn_p(i, s, l):
                dst = two(bank[s][0])
                if l == 1:
                    pe.wait_ge(heads_normed[s], i + 1)
                    src = heads_n[s]
                else:
                    pe.wait_ge(exp_made[s], FIRST + i * len(ONE_HEAD) + ONE_HEAD.index(l) + 1)
                    src = prob[s]
                for c in range(C):
                    for k in range(C):
                        mm = pe.transpose(dst[:, k, c * P:(c + 1) * P], src[:, c, k * P:(k + 1) * P], ident[:, :])
                mm.then_inc(p_turned[s], 1)

            def attend(i, s, l):
                dst = two(bank[s][1])
                pe.wait_ge(p_lo[s], FIRST + i * LAYERS + l + 1)
                if l != 1:
                    pe.wait_ge(proj_lo[s], FIRST + i * PROJS + PROJ[l, "v"])
                r_hi, r_lo = (hi_w["o1"], lo_w["o1"]) if l == 1 else (v_hi[s], v_lo[s])
                for c in range(C):
                    for k in range(C):
                        q = slice(c * P, (c + 1) * P)
                        mm = three(dst[:, c, :], pt_hi[s][:, k, q], pt_lo[s][:, k, q], r_hi[:, k, :], r_lo[:, k, :],
                                   k == 0, k == C - 1)
                mm.then_inc(attended[s], 1)

            def head_scores(i, s, h):
                dst = two(bank[s][0])
                if h == 0:
                    pe.wait_ge(q_stacked[s], (i + 1) * 16 * STACK_DMAS // 2)
                    pe.wait_ge(k_stacked[s], (i + 1) * 16 * STACK_DMAS // 2)
                else:
                    pe.wait_ge(max_found[s], i * SCORES + 1 + h)
                for c in range(C):
                    pe.matmul(dst[:, c, :], identb[:, :], mask[s][:, c, :], start=True, stop=False)
                    mm = pe.matmul(dst[:, c, :], q_stack[s][:, h, c * P:(c + 1) * P], k_stack[s][:, h, :],
                                   start=False, stop=True)
                mm.then_inc(scored[s], 1)

            def head_scores_t(i, s, h):
                dst = two(bank[s][1])
                pe.wait_ge(shift_made[s], i * HEADS + h + 1)
                if h:
                    pe.wait_ge(head_exp[s], i * HEADS + h)
                for k in range(C):
                    kk = slice(k * P, (k + 1) * P)
                    pe.matmul(dst[:, k, :], k_stack[s][:, h, kk], q_stack[s][:, h, :], start=True, stop=False)
                    for c in range(C):
                        mm = pe.matmul(dst[:, k, c * P:(c + 1) * P], shifted[s][:, h % 2, c, kk], identb[:, :],
                                       start=False, stop=(c == C - 1))
                mm.then_inc(scored_t[s], 1)

            def head_attend(i, s, h):
                dst = bank[s][2 + h % 2][:, 0:C * 3 * (HD + 1)].rearrange("p (c n) -> p c n", c=C)
                pe.wait_ge(head_lo[s], i * HEADS + h + 1)
                if h == 0:
                    pe.wait_ge(v3_made[s], i + 1)
                if h >= 2:
                    pe.wait_ge(head_read[s], i * HEADS + h - 1)
                for c in range(C):
                    for k in range(C):
                        q = slice(c * P, (c + 1) * P)
                        parts = v_parts[s][:, k, h].rearrange("p a d -> p (a d)")
                        pe.matmul(dst[:, c, :], ht_hi[s][:, h % 2, k, q], parts, start=(k == 0), stop=False)
                        mm = pe.matmul(dst[:, c, HD + 1:], ht_lo[s][:, h % 2, k, q], parts[:, HD + 1:],
                                       start=False, stop=(k == C - 1))
                mm.then_inc(head_done[s], 1)

            with pe.Fori(0, turns) as i:
                for l in range(LAYERS):
                    for s in range(SLOTS):
                        turn_x(i, s, l)
                    if l == 1:
                        for s in range(SLOTS):
                            begin(i, s, l)
                            project(i, s, l, "q", 1, "q1")
                            project(i, s, l, "k", 2, "k1")
                            values(i, s, l, 3, "v1")
                        for r in range(HEADS + 2):
                            for s in range(SLOTS):
                                if r < HEADS:
                                    head_scores(i, s, r)
                                if 1 <= r <= HEADS:
                                    head_scores_t(i, s, r - 1)
                                if r >= 2:
                                    head_attend(i, s, r - 2)
                    else:
                        for s in range(SLOTS):
                            g_and_v(i, s, l)
                        for s in range(SLOTS):
                            scores(i, s, l)
                    for s in range(SLOTS):
                        turn_p(i, s, l)
                    for s in range(SLOTS):
                        attend(i, s, l)

        @block.scalar
        def _(act):
            def xt_copy(i, s, l):
                act.wait_ge(x_turned[s], i * LAYERS + l + 1)
                src = two(bank[s][0])
                for c in range(C):
                    g = unit[:, 0, c:c + 1] if l == 0 else cc(f"g{l - 1}", c)
                    b = unit[:, 1, c:c + 1] if l == 0 else cc(f"b{l - 1}", c)
                    a = act.activation(xt[s][:, c, :], src[:, c, :], ACT.Identity, bias=b, scale=g)
                a.then_inc(xt_made[s], 1)

            def hi_copy(i, s, l, what, b, dst, bias=None):
                act.wait_ge(projected[s], i * PROJS + PROJ[l, what])
                src = two(bank[s][b])
                if bias is None:
                    a = act.activation(dst[:, :, :], src, ACT.Copy)
                else:
                    for c in range(C):
                        a = act.activation(dst[:, c, :], src[:, c, :], ACT.Identity, bias=cc(bias, c))
                a.then_inc(proj_hi[s], 1)

            def exps(i, s, l):
                act.wait_ge(max_found[s], i * SCORES + SCORE[l])
                src = two(bank[s][3])
                n = SCORE[l] - 1
                for c in range(C):
                    a = act.activation(prob[s][:, c, :], src[:, c, :], ACT.Exp, bias=neg_max[s][:, n, c:c + 1],
                                       accum_out=total[s][:, c:c + 1])
                a.then_inc(exp_made[s], 1)

            def turned_hi(i, s, l):
                act.wait_ge(p_turned[s], i * LAYERS + l + 1)
                act.activation(pt_hi[s][:, :, :], two(bank[s][0]), ACT.Copy).then_inc(p_hi[s], 1)

            def head_exps(i, s, h):
                act.wait_ge(scored_t[s], i * HEADS + h + 1)
                if h >= 2:
                    act.wait_ge(head_lo[s], i * HEADS + h - 1)
                    act.wait_ge(head_done[s], i * HEADS + h - 1)
                act.activation(ht_hi[s][:, h % 2], two(bank[s][1]), ACT.Exp)
                act.activation(ht[s][:, h % 2], two(bank[s][1]), ACT.Exp).then_inc(head_exp[s], 1)

            for s in range(SLOTS):
                act.sem_inc(exp_made[s], FIRST)
            act.wait_ge(weights_ready, 1)
            with act.Fori(0, turns) as i:
                for l in range(LAYERS):
                    for s in range(SLOTS):
                        xt_copy(i, s, l)
                    if l == 1:
                        for s in range(SLOTS):
                            hi_copy(i, s, l, "q", 1, g_hi[s], "bq1")
                            hi_copy(i, s, l, "k", 2, k_hi[s], "bk1")
                            act.wait_ge(projected[s], i * PROJS + PROJ[1, "v"])
                            act.activation(v_parts[s][:, :, :, 2, 0:HD],
                                           bank[s][3][:, :].rearrange("p (c h d) -> p c h d", c=C, h=HEADS),
                                           ACT.Copy).then_inc(proj_hi[s], 1)
                        for r in range(1, HEADS + 1):
                            for s in range(SLOTS):
                                head_exps(i, s, r - 1)
                    else:
                        for s in range(SLOTS):
                            hi_copy(i, s, l, "g", 1, g_hi[s], {2: "bqk2", 3: "bqk3"}.get(l))
                            hi_copy(i, s, l, "v", 2, v_hi[s])
                        for s in range(SLOTS):
                            exps(i, s, l)
                    for s in range(SLOTS):
                        turned_hi(i, s, l)

        @block.vector
        def _(dve):
            for s in range(SLOTS):
                for count in (mask_made, p_lo, summed, proj_lo):
                    dve.sem_inc(count[s], FIRST)
            dve.memset(unit[:, 0, :], 1.0).then_inc(const_made, 1)
            dve.memset(unit[:, 1, :], 0.0).then_inc(const_made, 1)
            dve.memset(half[:, :], -0.5).then_inc(const_made, 1)
            dve.memset(eps[:, :], EPS).then_inc(const_made, 1)
            for s in range(SLOTS):
                dve.memset(v_parts[s][:, :, :, :, HD:HD + 1], 0.0).then_inc(const_made, 1)
            dve.wait_ge(const_made, 4 + SLOTS)
            for s in range(SLOTS):
                dve.memset(v_parts[s][:, :, :, 2, HD:HD + 1], 1.0).then_inc(const_made, 1)
            dve.wait_ge(cols_in, 16)
            dve.tensor_copy(spread[:, 0, :], cc("bv1", 0).to_broadcast([P, P])).then_inc(spread_made, 1)
            dve.tensor_copy(spread[:, 1, :], cc("bv1", 1).to_broadcast([P, P])).then_inc(spread_made, 1)
            n1, n2, n3 = COLS.index("bq1"), COLS.index("bqk2"), COLS.index("bqk3")
            s1, s2 = HD ** -0.5, 128 ** -0.5
            dve.tensor_scalar(col[:, n1, :], col[:, n1, :], s1, None, ALU.mult)
            dve.tensor_scalar(col[:, n2, 0:1], col[:, n2, 0:1], s2, None, ALU.mult)
            dve.tensor_scalar(col[:, n3, 0:1], col[:, n3, 0:1], s2, None, ALU.mult)

            step = [0]

            def link(instruction):
                instruction.then_inc(prep_hi, 1)
                step[0] += 1
                dve.wait_ge(prep_hi, step[0])

            for m, name in enumerate(["qk_0", "vo_0", "qk_4", "vo_4"]):
                dve.wait_ge(prep_product, m + 1)
                a = two(bank[0][0])
                scale = D ** -0.5 if name.startswith("qk") else 1.0
                link(dve.tensor_scalar(hi_w[name][:, :, :], a, scale, None, ALU.mult))
                dve.scalar_tensor_tensor(lo_w[name][:, :, :], a, scale, hi_w[name][:, :, :].bitcast(F32),
                                         ALU.mult, ALU.subtract).then_inc(prep_chain, 1)
                dve.wait_ge(prep_chain, m + 1)
                dve.sem_inc(raw_split, 2)
            for n in range(8, len(RAW)):
                name = RAW[n]
                dve.wait_ge(raw_in[n % 4], 16 * (n // 4 + 1))
                a = stage[:, n % 4]
                parts = {"q1": ((0, D, s1),), "qk2": ((0, P, s2), (P, D, 1.0)), "qk3": ((0, P, s2), (P, D, 1.0))}
                for lo, hi, scale in parts.get(name, ((0, D, 1.0),)):
                    link(dve.tensor_scalar(hi_w[name][:, :, lo:hi], a[:, :, lo:hi], scale, None, ALU.mult))
                    last = dve.scalar_tensor_tensor(lo_w[name][:, :, lo:hi], a[:, :, lo:hi], scale,
                                                    hi_w[name][:, :, lo:hi].bitcast(F32), ALU.mult, ALU.subtract)
                    link(last)
                if name == "o1":
                    dve.wait_ge(bias_product, 1)
                dve.sem_inc(raw_split, 1)
            dve.sem_inc(weights_ready, 1)
            dve.wait_ge(rows_in, 16 * len(ROWS))
            link(dve.tensor_tensor(row["bo1"][:, :], bank[0][1][:, 0:D], row["bo1"][:, :], ALU.add))
            link(dve.tensor_tensor(row["b0"][:, :], row["b0"][:, :], row["bo1"][:, :], ALU.add))
            link(dve.tensor_tensor(row["b3"][:, :], row["b3"][:, :], row["bo4"][:, :], ALU.add))
            dve.sem_inc(rows_ready, 1)

            def xt_hi_part(i, s, l):
                dve.wait_ge(xt_made[s], i * LAYERS + l + 1)
                dve.tensor_copy(xt_hi[s][:, :, :], xt[s][:, :, :]).then_inc(xt_hi_made[s], 1)

            def lo_part(i, s, l, what, b, dst, hi, bias=None):
                dve.wait_ge(proj_hi[s], i * PROJS + PROJ[l, what])
                src = two(bank[s][b])
                if bias is None:
                    v = dve.tensor_tensor(dst[:, :, :], src, hi[:, :, :].bitcast(F32), ALU.subtract)
                else:
                    for c in range(C):
                        v = dve.scalar_tensor_tensor(dst[:, c, :], src[:, c, :], cc(bias, c),
                                                     hi[:, c, :].bitcast(F32), ALU.add, ALU.subtract)
                v.then_inc(proj_lo[s], 1)

            def row_max(i, s, number, b):
                dve.wait_ge(scored[s], FIRST + i * SCORES + number)
                dve.tensor_reduce(neg_max[s][:, number - 1, :], two(bank[s][b]), axis=AX.X, op=ALU.max,
                                  negate=True).then_inc(max_found[s], 1)

            def turned_lo(i, s, l):
                dve.wait_ge(p_hi[s], i * LAYERS + l + 1)
                dve.tensor_tensor(pt_lo[s][:, :, :], two(bank[s][0]), pt_hi[s][:, :, :].bitcast(F32),
                                  ALU.subtract).then_inc(p_lo[s], 1)

            def norm(i, s, l):
                src = two(bank[s][1])
                if l != 1:
                    a = ONE_HEAD.index(l)
                    dve.wait_ge(exp_made[s], FIRST + i * len(ONE_HEAD) + a + 1)
                    n = SCORE[l] - 1
                    dve.tensor_scalar(alive1[s][:, :], neg_max[s][:, n, :], 0.5 * BIG, None, ALU.is_lt).then_inc(inv_step[s], 1)
                    dve.reciprocal(scale_row[s][:, :], total[s][:, :]).then_inc(inv_step[s], 1)
                    dve.wait_ge(inv_step[s], i * 3 * len(ONE_HEAD) + 3 * a + 2)
                    factor = alive1[s][:, :] if l in (2, 3) else unit[:, 0, :]
                    dve.tensor_tensor(scale_row2[s][:, :], scale_row[s][:, :], factor, ALU.mult).then_inc(inv_step[s], 1)
                    dve.wait_ge(inv_step[s], i * 3 * len(ONE_HEAD) + 3 * a + 3)
                dve.wait_ge(attended[s], i * LAYERS + l + 1)
                dve.wait_ge(res_made[s], i * (LAYERS + 1) + l + 1)
                if l == 1:
                    v = dve.tensor_tensor(y[s][:, :, :], src, xres[s][:, :, :], ALU.add)
                else:
                    for c in range(C):
                        v = dve.scalar_tensor_tensor(y[s][:, c, :], src[:, c, :], scale_row2[s][:, c:c + 1],
                                                     xres[s][:, c, :], ALU.mult, ALU.add)
                v.then_inc(summed[s], 1)
                dve.wait_ge(summed[s], FIRST + i * LAYERS + l + 1)
                for c in range(C):
                    v = dve.bn_stats(stats[s][:, c, :], y[s][:, c, :])
                v.then_inc(stats_made[s], 1)
                dve.wait_ge(stats_made[s], i * LAYERS + l + 1)
                dve.memset(wait_cell[s][:, :], 0.0)
                for c in range(C):
                    v = dve.bn_aggr(mean_var[s][:, c, :], stats[s][:, c, :])
                v.then_inc(mean_made[s], 1)

            def center(i, s, l):
                dve.wait_ge(mean_made[s], i * LAYERS + l + 1)
                dve.wait_ge(rstd_made[s], i * LAYERS + l + 1)
                for c in range(C):
                    v = dve.tensor_scalar(y[s][:, c, :], y[s][:, c, :], mean_var[s][:, c, 0:1], rstd[s][:, c:c + 1],
                                          ALU.subtract, ALU.mult)
                v.then_inc(normed[s], 1)

            def shift(i, s, h):
                dve.wait_ge(max_found[s], i * SCORES + 2 + h)
                if h >= 2:
                    dve.wait_ge(scored_t[s], i * HEADS + h - 1)
                for c in range(C):
                    v = dve.tensor_scalar(shifted[s][:, h % 2, c, :], mask[s][:, c, :], neg_max[s][:, 1 + h, c:c + 1],
                                          None, ALU.add)
                v.then_inc(shift_made[s], 1)

            def head_sum(i, s, h):
                dve.wait_ge(head_done[s], i * HEADS + h + 1)
                src = bank[s][2 + h % 2][:, 0:C * 3 * (HD + 1)].rearrange("p (c a d) -> p c d a", c=C, a=3)
                dve.tensor_reduce(head_out[s][:, :, h, :], src, axis=AX.X, op=ALU.add).then_inc(head_read[s], 1)

            dve.wait_ge(const_made, 4 + 2 * SLOTS)
            with dve.Fori(0, turns) as i:
                for s in range(SLOTS):
                    dve.wait_ge(adj_in[s], (i + 1) * 16)
                    dve.wait_ge(scored[s], FIRST + i * SCORES)
                    dve.tensor_scalar(mask[s][:, :, :], adj_sb[s][:, :, :], 0.0, -BIG, ALU.is_equal,
                                      ALU.mult).then_inc(mask_made[s], 1)
                for l in range(LAYERS):
                    for s in range(SLOTS):
                        xt_hi_part(i, s, l)
                    if l == 1:
                        for s in range(SLOTS):
                            lo_part(i, s, l, "q", 1, g_lo[s], g_hi[s], "bq1")
                            lo_part(i, s, l, "k", 2, k_lo[s], k_hi[s], "bk1")
                            dve.wait_ge(proj_hi[s], i * PROJS + PROJ[1, "v"])
                            dve.tensor_tensor(v_rest[s][:, :, :].rearrange("p c (h d) -> p c h d", h=HEADS),
                                              bank[s][3][:, :].rearrange("p (c h d) -> p c h d", c=C, h=HEADS),
                                              v_parts[s][:, :, :, 2, 0:HD], ALU.subtract).then_inc(proj_lo[s], 1)
                        for r in range(HEADS + 2):
                            for s in range(SLOTS):
                                if r < HEADS:
                                    row_max(i, s, 2 + r, 0)
                                    shift(i, s, r)
                                if r >= 2:
                                    head_sum(i, s, r - 2)
                        for s in range(SLOTS):
                            dve.tensor_scalar(alive[s][:, :, :], neg_max[s][:, 1:1 + HEADS, :].rearrange("p h c -> p c h"),
                                              0.5 * BIG, None, ALU.is_lt).then_inc(heads_chain[s], 1)
                            dve.wait_ge(head_read[s], (i + 1) * HEADS)
                            dve.wait_ge(heads_chain[s], i * 3 + 1)
                            dve.tensor_tensor(den[s][:, :, :], head_out[s][:, :, :, HD], alive[s][:, :, :],
                                              ALU.mult).then_inc(heads_chain[s], 1)
                            dve.wait_ge(heads_chain[s], i * 3 + 2)
                            dve.reciprocal(inv[s][:, :, :], den[s][:, :, :]).then_inc(heads_chain[s], 1)
                            dve.wait_ge(heads_chain[s], i * 3 + 3)
                            for c in range(C):
                                v = dve.tensor_tensor(heads_n[s][:, c, :].rearrange("p (h d) -> p h d", h=HEADS),
                                                      head_out[s][:, c, :, 0:HD],
                                                      inv[s][:, c, :].unsqueeze(2).to_broadcast([P, HEADS, HD]), ALU.mult)
                            v.then_inc(heads_normed[s], 1)
                    else:
                        for s in range(SLOTS):
                            lo_part(i, s, l, "g", 1, g_lo[s], g_hi[s], {2: "bqk2", 3: "bqk3"}.get(l))
                            lo_part(i, s, l, "v", 2, v_lo[s], v_hi[s])
                        for s in range(SLOTS):
                            row_max(i, s, SCORE[l], 3)
                    for s in range(SLOTS):
                        turned_lo(i, s, l)
                    for s in range(SLOTS):
                        norm(i, s, l)
                    for s in range(SLOTS):
                        center(i, s, l)

        @block.gpsimd
        def _(pool):
            pool.memset(ident[:, :], 0.0).then_inc(ident_made, 1)
            for s in range(SLOTS):
                pool.sem_inc(x_used[s], FIRST)
            pool.wait_ge(ident_made, 1)
            pool.affine_select(out=ident[:, :], in_=ident[:, :], compare_op=ALU.not_equal, fill=1.0, base=0,
                               pattern=[[-1, P]], channel_multiplier=1).then_inc(ident_made, 1)
            pool.wait_ge(ident_made, 2)
            pool.tensor_copy(identb[:, :], ident[:, :]).then_inc(ident_made, 1)
            pool.wait_ge(rows_ready, 1)
            pool.wait_ge(const_made, 4)

            def residual(i, s, l):
                if l == 0:
                    pool.wait_ge(x_in[s], (i + 1) * 16)
                    pool.wait_ge(summed[s], FIRST + i * LAYERS)
                    pool.tensor_tensor(xres[s][:, :, :], xin[s][:, :, :],
                                       row["bo0"][:, :].unsqueeze(1).to_broadcast([P, C, D]), ALU.add).then_inc(res_made[s], 1)
                    pool.wait_ge(res_made[s], i * (LAYERS + 1) + 1)
                    pool.wait_ge(x_turned[s], i * LAYERS + 1)
                    pool.sem_inc(x_used[s], 1)
                    return
                pool.wait_ge(normed[s], i * LAYERS + l)
                if l == LAYERS:
                    pool.wait_ge(stored[s], (i + 1) * 16)
                dst = result[s] if l == LAYERS else xres[s]
                pool.tensor_tensor(dst[:, :, :], y[s][:, :, :],
                                   row[f"g{l - 1}"][:, :].unsqueeze(1).to_broadcast([P, C, D]), ALU.mult).then_inc(scaled_up[s], 1)
                pool.wait_ge(scaled_up[s], i * LAYERS + l)
                pool.tensor_tensor(dst[:, :, :], dst[:, :, :],
                                   row[f"b{l - 1}"][:, :].unsqueeze(1).to_broadcast([P, C, D]), ALU.add).then_inc(res_made[s], 1)

            with pool.Fori(0, turns) as i:
                for l in range(LAYERS):
                    for s in range(SLOTS):
                        if l == 0:
                            residual(i, s, 0)
                        pool.wait_ge(xt_hi_made[s], i * LAYERS + l + 1)
                        pool.tensor_tensor(xt_lo[s][:, :, :], xt[s][:, :, :], xt_hi[s][:, :, :].bitcast(F32),
                                           ALU.subtract).then_inc(xt_lo_made[s], 1)
                    if l > 0:
                        for s in range(SLOTS):
                            residual(i, s, l)
                    if l == 1:
                        for s in range(SLOTS):
                            pool.wait_ge(proj_lo[s], FIRST + i * PROJS + PROJ[1, "v"])
                            rest = v_rest[s][:, :, :].rearrange("p c (h d) -> p c h d", h=HEADS)
                            for c in range(C):
                                v = pool.tensor_tensor(v_parts[s][:, c, :, 1, 0:HD], rest[:, c],
                                                       unit[:, 0, 0:1].unsqueeze(2).to_broadcast([P, HEADS, HD]), ALU.mult)
                            v.then_inc(v2_made[s], 1)
                            pool.wait_ge(v2_made[s], i + 1)
                            for c in range(C):
                                v = pool.tensor_tensor(v_parts[s][:, c, :, 0, 0:HD], rest[:, c], v_parts[s][:, c, :, 1, 0:HD], ALU.subtract)
                            v.then_inc(v3_made[s], 1)
                        for h in range(HEADS):
                            for s in range(SLOTS):
                                pool.wait_ge(head_exp[s], i * HEADS + h + 1)
                                if h >= 2:
                                    pool.wait_ge(head_done[s], i * HEADS + h - 1)
                                pool.tensor_tensor(ht_lo[s][:, h % 2], ht[s][:, h % 2], ht_hi[s][:, h % 2],
                                                   ALU.subtract).then_inc(head_lo[s], 1)
                    for s in range(SLOTS):
                        pool.wait_ge(mean_made[s], i * LAYERS + l + 1)
                        pool.tensor_tensor(var_eps[s][:, :], mean_var[s][:, :, 1], eps[:, :], ALU.add).then_inc(eps_added[s], 1)
                        pool.wait_ge(eps_added[s], i * LAYERS + l + 1)
                        pool.tensor_tensor(rstd[s][:, :], var_eps[s][:, :], half[:, :], ALU.pow).then_inc(rstd_made[s], 1)
                for s in range(SLOTS):
                    residual(i, s, LAYERS)


def kernel(x, adj, L0_gnn_Wq, L0_gnn_Wk, L0_gnn_Wv, L0_gnn_Wo, L0_gnn_bo, L0_gnn_gamma, L0_gnn_beta,
           L1_gnn_Wq, L1_gnn_bq, L1_gnn_Wk, L1_gnn_bk, L1_gnn_Wv, L1_gnn_bv, L1_gnn_Wo, L1_gnn_bo, L1_gnn_gamma,
           L1_gnn_beta, L2_gnn_Wq, L2_gnn_bq, L2_gnn_Wk, L2_gnn_bk, L2_gnn_Wc, L2_gnn_ln_g, L2_gnn_ln_b,
           L3_gnn_Wq, L3_gnn_Wk, L3_gnn_Wv, L3_gnn_Wo, L3_gnn_bo, L3_gnn_gamma, L3_gnn_beta):
    import numpy as np
    import concourse.bacc as bacc
    from concourse import mybir as mb
    from concourse.bass_utils import run_bass_kernel_spmd

    a = np.asarray
    qk2 = [np.concatenate([a(L2_gnn_Wq)[k].T, a(L2_gnn_Wk)[k].T], axis=1) for k in range(2)]
    weights = np.stack([a(L0_gnn_Wq).T, a(L0_gnn_Wk).T, a(L0_gnn_Wv).T, a(L0_gnn_Wo),
                        a(L3_gnn_Wq).T, a(L3_gnn_Wk).T, a(L3_gnn_Wv).T, a(L3_gnn_Wo),
                        a(L1_gnn_Wq), a(L1_gnn_Wk), a(L1_gnn_Wv), a(L1_gnn_Wo), qk2[0], qk2[1],
                        a(L2_gnn_Wc)[0].T, a(L2_gnn_Wc)[1].T])
    g = [a(L0_gnn_gamma), a(L1_gnn_gamma), a(L2_gnn_ln_g)[0], a(L2_gnn_ln_g)[1], a(L3_gnn_gamma)]
    b = [a(L0_gnn_beta), a(L1_gnn_beta), a(L2_gnn_ln_b)[0], a(L2_gnn_ln_b)[1], a(L3_gnn_beta)]
    rows = np.stack(g + b + [a(L0_gnn_bo), a(L1_gnn_bo), a(L3_gnn_bo)])
    rows = np.ascontiguousarray(np.broadcast_to(rows, (128,) + rows.shape))
    bqk2 = [np.concatenate([a(L2_gnn_bq)[k], a(L2_gnn_bk)[k]]) for k in range(2)]
    cols = np.stack(g[:4] + b[:4] + [a(L1_gnn_bq), a(L1_gnn_bk), a(L1_gnn_bv)] + bqk2)
    cols = cols.reshape(len(cols), 2, 128).transpose(2, 0, 1)
    given = {"x": a(x), "adj": a(adj), "weights": weights, "rows": rows, "cols": cols}

    nc = bacc.Bacc("TRN2", target_bir_lowering=False, num_devices=1)
    arrays, args = {}, []
    for name, v in given.items():
        arrays[f"in_{name}"] = v = np.ascontiguousarray(v)
        args.append(nc.dram_tensor(f"in_{name}", v.shape, mb.dt.from_np(v.dtype), kind="ExternalInput").ap())
    args.append(nc.dram_tensor("out_0", given["x"].shape, mb.dt.float32, kind="ExternalOutput").ap())
    graph_stack_kernel(nc, *args)
    return run_bass_kernel_spmd(nc, [arrays], core_ids=[0]).results[0]["out_0"]
```

```python
from contextlib import ExitStack

import concourse.bass as bass
from concourse import mybir

P = 128
N = 256
D = 256
C = N // P
HEADS = 8
HD = D // HEADS
LAYERS = 5
ONE_HEAD = [0, 2, 3, 4]
PAIR = 2
SLOTS = 2 * PAIR
QUARTERS = 4
BIG = 1.0e30
EPS = 1e-5
FIRST = 1

F32 = mybir.dt.float32
F32R = mybir.dt.float32r
F16 = mybir.dt.float16
BF16 = mybir.dt.bfloat16
I32 = mybir.dt.int32
ALU = mybir.AluOpType
ACT = mybir.ActivationFunctionType
AX = mybir.AxisListType

RAW = ["q0T", "k0T", "v0T", "o0", "q3T", "k3T", "v3T", "o3", "q1", "k1", "v1", "qk2", "qk3", "c2", "c3", "o1"]
STAGED = len(RAW) - 1
USED = ["qk_0", "vo_0", "q1", "k1", "v1", "qk2", "c2", "qk3", "c3", "qk_4", "vo_4"]
ROWS = ["g0", "g1", "g2", "g3", "g4", "b0", "b1", "b2", "b3", "b4", "bo0", "bo1", "bo4"]
COLS = ["g0", "g1", "g2", "g3", "b0", "b1", "b2", "b3", "bq1", "bk1", "bv1", "bqk2", "bqk3"]

YOUNG, OLD = "young", "old"
ORDER = [
    (YOUNG, "turn", 0), (OLD, "turn", 2), (YOUNG, "project", 0), (OLD, "project", 2),
    (YOUNG, "score", 0), (OLD, "score", 2), (YOUNG, "probs", 0), (OLD, "probs", 2),
    (YOUNG, "attend", 0), (OLD, "attend", 2), (YOUNG, "norm", 0), (OLD, "norm", 2),
    (YOUNG, "turn", 1), (OLD, "turn", 3), (YOUNG, "project", 1), (OLD, "project", 3),
    (OLD, "score", 3), (YOUNG, "round", 0), (OLD, "probs", 3), (YOUNG, "round", 1), (OLD, "attend", 3),
    (YOUNG, "round", 2), (OLD, "norm", 3), (YOUNG, "round", 3), (OLD, "turn", 4), (YOUNG, "round", 4),
    (OLD, "project", 4), (YOUNG, "round", 5), (OLD, "score", 4), (YOUNG, "round", 6), (OLD, "probs", 4),
    (YOUNG, "round", 7), (OLD, "attend", 4), (YOUNG, "round", 8), (OLD, "norm", 4), (YOUNG, "round", 9),
    (YOUNG, "probs", 1), (YOUNG, "attend", 1), (YOUNG, "norm", 1),
]


def head_of(r):
    return r // 2 + 4 * (r % 2)


def half_turn(steps, young, old):
    for who, step, n in ORDER:
        at = young if who == YOUNG else old
        if at is not None and step in steps:
            steps[step](at[0] * PAIR, at[1], n)


def all_turns(engine, turns, steps, before=None):
    def half(young, old):
        if before is not None:
            before(young, old)
        half_turn(steps, young, old)
    half((0, 0), None)
    with engine.Fori(0, turns - 1) as i:
        half((1, i), (0, i))
        half((0, i + 1), (1, i))
    half((1, turns - 1), (0, turns - 1))
    half(None, (1, turns - 1))


def graph_stack_kernel(nc, x, adj, weights, rows, cols, out):
    graphs = x.shape[0]
    turns = graphs // SLOTS
    with ExitStack() as ctx:
        def sb(name, shape, dt=F32):
            return ctx.enter_context(nc.sbuf_tensor(name, [P] + shape, dt))

        def per_slot(name, shape, dt=F32):
            return [sb(f"{name}{s}", shape, dt) for s in range(SLOTS)]

        def per_seat(name, shape, dt=F32):
            return [sb(f"{name}{j}", shape, dt) for j in range(PAIR)] * 2

        def sem(name):
            return ctx.enter_context(nc.semaphore(name))

        def sems(name):
            return [sem(f"{name}{s}") for s in range(SLOTS)]

        def seat_sems(name):
            return [sem(f"{name}{j}") for j in range(PAIR)] * 2

        ident = sb("ident", [P])
        identb = sb("identb", [P], BF16)
        hi_w = {n: sb(f"wh_{n}", [C, D], F32R) for n in USED}
        lo_w = {n: sb(f"wl_{n}", [C, D], F32R) for n in USED}
        o1 = sb("o1", [C, D])
        row = {n: sb(f"row_{n}", [D]) for n in ROWS if n not in ("bo1", "bo4")}
        col = sb("col", [len(COLS), C])
        unit = sb("unit", [2, C])
        half = sb("half", [C])
        eps = sb("eps", [C])

        mask = per_slot("mask", [C, N], BF16)
        xres = per_slot("xres", [C, D])
        xt_hi = per_slot("xt_hi", [C, N], F32R)
        xt_lo = per_slot("xt_lo", [C, N], F32R)
        g_hi = per_slot("g_hi", [C, N], F32R)
        g_lo = per_slot("g_lo", [C, N], F32R)
        v = per_slot("v", [C, D])
        stage = v
        prob = per_slot("prob", [C, N])
        qk = prob
        pt = per_slot("pt", [C, N])
        xt = pt
        y = per_slot("y", [C, D])
        row["bo1"], row["bo4"] = y[SLOTS - 1][:, 0, :], y[SLOTS - 1][:, 1, :]
        neg_max = per_slot("neg_max", [LAYERS, C])
        total = per_slot("total", [C])
        alive1 = per_slot("alive1", [C])
        inv_total = per_slot("inv_total", [C])
        row_scale = per_slot("row_scale", [C])
        stats = per_slot("stats", [C, 6])
        mean_var = per_slot("mean_var", [C, 2])
        var_eps = per_slot("var_eps", [C])
        rstd = per_slot("rstd", [C])
        wait_cell = per_slot("wait_cell", [1])

        xin = per_seat("xin", [C, D])
        adj_sb = per_seat("adj_sb", [C, N], I32)
        parts = per_seat("parts", [4, C, N], F32R)
        stack = per_seat("stack", [2, 2, 2, N], F32R)
        v_parts = per_seat("v_parts", [C, HEADS, 3, HD + 1], BF16)
        shifted = per_seat("shifted", [2, C, N], BF16)
        ht_hi = per_seat("ht_hi", [2, C, N], F16)
        ht_lo = per_seat("ht_lo", [2, C, N], F16)
        ht = per_seat("ht", [2, C, N])
        head_out = per_seat("head_out", [C, HEADS, HD + 1])
        head_max = per_seat("head_max", [HEADS, C])
        alive = per_seat("alive", [C, HEADS])
        den = per_seat("den", [C, HEADS])
        inv = per_seat("inv", [C, HEADS])

        bank = [[ctx.enter_context(nc.psum_tensor(f"bank{s}{b}", [P, 512], F32)) for b in range(2)]
                for s in range(SLOTS)]

        def two(s, b):
            return bank[s][b][:, :].rearrange("p (c n) -> p c n", c=C)

        def by_part(s):
            return bank[s][0][:, 0:C * 3 * (HD + 1)].rearrange("p (c n) -> p c n", c=C)

        cols_in, rows_in, ident_made, o1_in = sem("cols_in"), sem("rows_in"), sem("ident_made"), sem("o1_in")
        raw_in = [sem(f"raw_in{k}") for k in range(4)]
        raw_split, prep_product, prep_part = sem("raw_split"), sem("prep_product"), sem("prep_part")
        prep_read, weights_ready = sem("prep_read"), sem("weights_ready")
        const_made, rows_ready, spread_made, bias_product = sem("const_made"), sem("rows_ready"), sem("spread_made"), sem("bias_product")
        turned, xt_hi_made = sems("turned"), sems("xt_hi_made")
        xt_lo_made, pt_made, attended = sems("xt_lo_made"), sems("pt_made"), sems("attended")
        g_product, g_hi_made, g_made = sems("g_product"), sems("g_hi_made"), sems("g_made")
        v_product, v_made = sems("v_product"), sems("v_made")
        mask_made = sems("mask_made")
        scored, max_found, exp_made = sems("scored"), sems("max_found"), sems("exp_made")
        inv_made = sems("inv_made")
        summed = sems("summed")
        mean_made, rstd_made, normed = sems("mean_made"), sems("rstd_made"), sems("normed")
        norm_step = sems("norm_step")
        res_made, stored = sems("res_made"), sems("stored")
        x_in, x_used, adj_in, adj_used = seat_sems("x_in"), seat_sems("x_used"), seat_sems("adj_in"), seat_sems("adj_used")
        qk_product, qk_hi_made, qk_lo_made = seat_sems("qk_product"), seat_sems("qk_hi_made"), seat_sems("qk_lo_made")
        v1_product, va_made, rest_made, vc_made = seat_sems("v1_product"), seat_sems("va_made"), seat_sems("rest_made"), seat_sems("vc_made")
        stacked = [[sem(f"stacked{j}_{k}") for k in range(2)] for j in range(PAIR)] * 2
        head_scored, head_maxed, shift_made = seat_sems("head_scored"), seat_sems("head_maxed"), seat_sems("shift_made")
        scored_t, head_exp, head_lo = seat_sems("scored_t"), seat_sems("head_exp"), seat_sems("head_lo")
        head_done, head_read = seat_sems("head_done"), seat_sems("head_read")
        heads_normed = seat_sems("heads_normed")

        block = ctx.enter_context(nc.Block())

        def cc(name, c):
            return col[:, COLS.index(name), c:c + 1]

        def use(s, i):
            return i * 2 + s // PAIR

        @block.sync
        def _(sp):
            for s in range(SLOTS):
                sp.sem_inc(stored[s], 16)
            sp.dma_start(col[:, :, :], cols).then_inc(cols_in, 16)

            def load(s, i):
                u = use(s, i)
                sp.wait_ge(x_used[s], FIRST + u)
                sp.dma_start(xin[s][:, :, :], x[i * SLOTS + s].rearrange("(c p) d -> p c d", p=P)).then_inc(x_in[s], 16)
                sp.wait_ge(adj_used[s], FIRST + u)
                sp.dma_start(adj_sb[s][:, :, :], adj[i * SLOTS + s].rearrange("(c p) d -> p c d", p=P)).then_inc(adj_in[s], 16)

            for n in range(STAGED):
                if n >= 4:
                    sp.wait_ge(raw_split, n - 3)
                sp.dma_start(stage[n % 4][:, :, :], weights[n].rearrange("(c p) n -> p c n", p=P)).then_inc(raw_in[n % 4], 16)
                if n == 3:
                    sp.dma_start(o1[:, :, :], weights[STAGED].rearrange("(c p) n -> p c n", p=P)).then_inc(o1_in, 16)
                    for s in range(PAIR):
                        load(s, 0)
            for m, r in enumerate(ROWS):
                sp.dma_start(row[r] if r in ("bo1", "bo4") else row[r][:, :], rows[:, m, :]).then_inc(rows_in, 16)

            def stack_quarters(s0, i):
                for q in range(QUARTERS):
                    for s in range(s0, s0 + PAIR):
                        u = use(s, i)
                        if q == 0:
                            sp.wait_ge(qk_lo_made[s], 2 * u + 2)
                        sp.wait_ge(scored_t[s], FIRST + u * HEADS + (2 * (q - 1) if q >= 2 else 0))
                        for part, (first, step) in enumerate(((0, 2), (0, 3), (1, 1), (1, 2))):
                            sp.dma_start(stack[s][32 * part:32 * part + 32, q % 2].bitcast(F32),
                                         parts[s][32 * q:32 * q + 32, first:first + step + 1:step].bitcast(F32)
                                         ).then_inc(stacked[s][q % 2], 16)

            def store(s0, i):
                for s in range(s0, s0 + PAIR):
                    sp.wait_ge(res_made[s], FIRST + (i + 1) * (LAYERS + 1))
                    sp.dma_start(out[i * SLOTS + s].rearrange("(c p) d -> p c d", p=P), xres[s][:, :, :]).then_inc(stored[s], 16)

            def next_load(s0, i):
                for s in range(s0, s0 + PAIR):
                    load(s, i)

            stack_quarters(0, 0)
            next_load(PAIR, 0)
            with sp.Fori(0, turns - 1) as i:
                stack_quarters(PAIR, i)
                next_load(0, i + 1)
                store(0, i)
                stack_quarters(0, i + 1)
                next_load(PAIR, i + 1)
                store(PAIR, i)
            stack_quarters(PAIR, turns - 1)
            store(0, turns - 1)
            store(PAIR, turns - 1)
            for s in range(SLOTS):
                sp.wait_ge(stored[s], 16 * (turns + 1))

        @block.tensor
        def _(pe):
            for s in range(SLOTS):
                pe.sem_inc(scored[s], FIRST)
            for j in range(PAIR):
                pe.sem_inc(scored_t[j], FIRST)
            for m in range(4):
                a, b = (2 * m) % 4, (2 * m + 1) % 4
                pe.wait_ge(raw_in[a], 16 * (m // 2 + 1))
                pe.wait_ge(raw_in[b], 16 * (m // 2 + 1))
                if m:
                    pe.wait_ge(prep_read, m)
                for c in range(C):
                    for e in range(C):
                        mm = pe.matmul(two(0, 0)[:, c, :], stage[a][:, e, c * P:(c + 1) * P], stage[b][:, e, :],
                                       start=(e == 0), stop=(e == C - 1))
                mm.then_inc(prep_product, 1)
            pe.wait_ge(spread_made, 2)
            pe.wait_ge(o1_in, 16)
            for e in range(C):
                mm = pe.matmul(bank[0][1][:, 0:D], prob[0][:, e, 0:P], o1[:, e, :], start=(e == 0), stop=(e == C - 1))
            mm.then_inc(bias_product, 1)
            pe.wait_ge(ident_made, 3)
            pe.wait_ge(weights_ready, 1)
            pe.wait_ge(rows_ready, 1)

            def three(dst, l_hi, l_lo, r_hi, r_lo, first, last):
                pe.matmul(dst, l_hi, r_hi, start=first, stop=False)
                pe.matmul(dst, l_hi, r_lo, start=False, stop=False)
                return pe.matmul(dst, l_lo, r_hi, start=False, stop=last)

            def transposed_product(s, b, weight):
                dst, h, w = two(s, b), hi_w[weight], lo_w[weight]
                for c in range(C):
                    for d in range(C):
                        k = slice(c * P, (c + 1) * P)
                        mm = three(dst[:, c, :], h[:, d, k], w[:, d, k], xt_hi[s][:, d, :], xt_lo[s][:, d, :],
                                   d == 0, d == C - 1)
                return mm

            def product(s, b, weight):
                dst, h, w = two(s, b), hi_w[weight], lo_w[weight]
                for c in range(C):
                    for d in range(C):
                        k = slice(c * P, (c + 1) * P)
                        mm = three(dst[:, c, :], xt_hi[s][:, d, k], xt_lo[s][:, d, k], h[:, d, :], w[:, d, :],
                                   d == 0, d == C - 1)
                return mm

            def turn(s0, i, l):
                for s in range(s0, s0 + PAIR):
                    dst = two(s, 0)
                    if l == 0:
                        pe.wait_ge(x_in[s], (use(s, i) + 1) * 16)
                        pe.wait_ge(pt_made[s], FIRST + i * LAYERS)
                    else:
                        pe.wait_ge(normed[s], i * LAYERS + l)
                    src = xin[s] if l == 0 else y[s]
                    for c in range(C):
                        for d in range(C):
                            mm = pe.transpose(dst[:, d, c * P:(c + 1) * P], src[:, c, d * P:(d + 1) * P], ident[:, :])
                    mm.then_inc(turned[s], 1)

            def project(s0, i, l):
                for s in range(s0, s0 + PAIR):
                    pe.wait_ge(xt_hi_made[s], 2 * (i * LAYERS + l + 1))
                    pe.wait_ge(xt_lo_made[s], i * LAYERS + l + 1)
                    if l == 0:
                        pe.wait_ge(summed[s], FIRST + i * 2 * LAYERS)
                    if l == 1:
                        transposed_product(s, 1, "q1").then_inc(qk_product[s], 1)
                        transposed_product(s, 0, "k1").then_inc(qk_product[s], 1)
                    else:
                        transposed_product(s, 1, {0: "qk_0", 2: "qk2", 3: "qk3", 4: "qk_4"}[l]).then_inc(g_product[s], 1)
                        product(s, 0, {0: "vo_0", 2: "c2", 3: "c3", 4: "vo_4"}[l]).then_inc(v_product[s], 1)
                if l == 1:
                    for s in range(s0, s0 + PAIR):
                        pe.wait_ge(qk_lo_made[s], 2 * use(s, i) + 1)
                        product(s, 1, "v1").then_inc(v1_product[s], 1)

            def score(s0, i, l):
                for s in range(s0, s0 + PAIR):
                    dst = two(s, 1)
                    pe.wait_ge(g_made[s], i * len(ONE_HEAD) + ONE_HEAD.index(l) + 1)
                    if l == 0:
                        pe.wait_ge(mask_made[s], i + 1)
                    for c in range(C):
                        k = slice(c * P, (c + 1) * P)
                        pe.matmul(dst[:, c, :], identb[:, :], mask[s][:, c, :], start=True, stop=False)
                        if l in (0, 4):
                            for e in range(C):
                                mm = three(dst[:, c, :], g_hi[s][:, e, k], g_lo[s][:, e, k], xt_hi[s][:, e, :],
                                           xt_lo[s][:, e, :], False, e == C - 1)
                        else:
                            mm = pe.matmul(dst[:, c, :], qk[s][:, 0, k], qk[s][:, 1, :], start=False, stop=True)
                    mm.then_inc(scored[s], 1)

            def probs(s0, i, l):
                for s in range(s0, s0 + PAIR):
                    dst = two(s, 0)
                    if l == 1:
                        pe.wait_ge(heads_normed[s], 4 * use(s, i) + 4)
                    else:
                        a = i * len(ONE_HEAD) + ONE_HEAD.index(l) + 1
                        pe.wait_ge(v_made[s], a)
                        pe.wait_ge(exp_made[s], a)
                    for c in range(C):
                        for k in range(C):
                            mm = pe.transpose(dst[:, k, c * P:(c + 1) * P], prob[s][:, c, k * P:(k + 1) * P], ident[:, :])
                    mm.then_inc(turned[s], 1)

            def attend(s0, i, l):
                for s in range(s0, s0 + PAIR):
                    dst = two(s, 1)
                    pe.wait_ge(pt_made[s], FIRST + i * LAYERS + l + 1)
                    right = o1 if l == 1 else v[s]
                    for c in range(C):
                        for k in range(C):
                            mm = pe.matmul(dst[:, c, :], pt[s][:, k, c * P:(c + 1) * P], right[:, k, :],
                                           start=(k == 0), stop=(k == C - 1))
                    mm.then_inc(attended[s], 1)

            def round_(s0, i, r):
                for s in range(s0, s0 + PAIR):
                    if r >= HEADS:
                        continue
                    u = use(s, i)
                    dst, q = two(s, 0), r // 2
                    if r % 2 == 0:
                        pe.wait_ge(stacked[s][q % 2], u * 128 + 64 * (q // 2) + 64)
                    if r == 1 or r == 2:
                        pe.wait_ge(head_maxed[s], u * HEADS + r)
                    if r >= 3:
                        pe.wait_ge(head_read[s], u * HEADS + r - 2)
                    for c in range(C):
                        pe.matmul(dst[:, c, :], identb[:, :], mask[s][:, c, :], start=True, stop=False)
                        mm = pe.matmul(dst[:, c, :], stack[s][:, q % 2, 0, r % 2, c * P:(c + 1) * P],
                                       stack[s][:, q % 2, 1, r % 2, :], start=False, stop=True)
                    mm.then_inc(head_scored[s], 1)
                for s in range(s0, s0 + PAIR):
                    if not 1 <= r <= HEADS:
                        continue
                    u, h = use(s, i), r - 1
                    dst, place, w = two(s, 1), (h // 2) % 2, h % 2
                    pe.wait_ge(shift_made[s], u * HEADS + h + 1)
                    if h == 0:
                        pe.wait_ge(rest_made[s], u + 1)
                    else:
                        pe.wait_ge(head_exp[s], u * HEADS + h)
                    for k in range(C):
                        kk = slice(k * P, (k + 1) * P)
                        pe.matmul(dst[:, k, :], stack[s][:, place, 1, w, kk], stack[s][:, place, 0, w, :],
                                  start=True, stop=False)
                        for c in range(C):
                            mm = pe.matmul(dst[:, k, c * P:(c + 1) * P], shifted[s][:, h % 2, c, kk], identb[:, :],
                                           start=False, stop=(c == C - 1))
                    mm.then_inc(scored_t[s], 1)
                for s in range(s0, s0 + PAIR):
                    if r < 2:
                        continue
                    u, h = use(s, i), r - 2
                    dst = by_part(s)
                    pe.wait_ge(head_lo[s], u * HEADS + h + 1)
                    if h == 0:
                        pe.wait_ge(vc_made[s], 2 * u + 2)
                    if r < HEADS:
                        pe.wait_ge(head_maxed[s], u * HEADS + r + 1)
                    else:
                        pe.wait_ge(head_read[s], u * HEADS + h)
                    for c in range(C):
                        for k in range(C):
                            q = slice(c * P, (c + 1) * P)
                            right = v_parts[s][:, k, head_of(h)].rearrange("p a d -> p (a d)")
                            pe.matmul(dst[:, c, :], ht_hi[s][:, h % 2, k, q], right, start=(k == 0), stop=False)
                            mm = pe.matmul(dst[:, c, HD + 1:], ht_lo[s][:, h % 2, k, q], right[:, HD + 1:],
                                           start=False, stop=(k == C - 1))
                    mm.then_inc(head_done[s], 1)

            all_turns(pe, turns, {"turn": turn, "project": project, "score": score, "probs": probs,
                                  "attend": attend, "round": round_})

        @block.scalar
        def _(act):
            def turn(s0, i, l):
                for s in range(s0, s0 + PAIR):
                    act.wait_ge(turned[s], 2 * (i * LAYERS + l) + 1)
                    for c in range(C):
                        g = unit[:, 0, c:c + 1] if l == 0 else cc(f"g{l - 1}", c)
                        b = unit[:, 1, c:c + 1] if l == 0 else cc(f"b{l - 1}", c)
                        a = act.activation(xt[s][:, c, :], two(s, 0)[:, c, :], ACT.Identity, bias=b, scale=g)
                    a.then_inc(xt_hi_made[s], 1)
                    act.wait_ge(xt_hi_made[s], 2 * (i * LAYERS + l) + 1)
                    act.activation(xt_hi[s][:, :, :], xt[s][:, :, :], ACT.Copy).then_inc(xt_hi_made[s], 1)

            def project(s0, i, l):
                for s in range(s0, s0 + PAIR):
                    u = use(s, i)
                    n = i * len(ONE_HEAD) + (ONE_HEAD.index(l) + 1 if l != 1 else 0)
                    if l == 1:
                        for k, bias in ((0, "bq1"), (2, "bk1")):
                            act.wait_ge(qk_product[s], 2 * u + 1 + k // 2)
                            for c in range(C):
                                a = act.activation(parts[s][:, k, c, :], two(s, 1 - k // 2)[:, c, :], ACT.Identity,
                                                   bias=cc(bias, c))
                            a.then_inc(qk_hi_made[s], 1)
                        continue
                    act.wait_ge(g_product[s], n)
                    if l in (0, 4):
                        act.activation(g_hi[s][:, :, :], two(s, 1), ACT.Copy).then_inc(g_hi_made[s], 1)
                    else:
                        for c in range(C):
                            a = act.activation(qk[s][:, c, :], two(s, 1)[:, c, :], ACT.Identity,
                                               bias=cc(f"bqk{l}", c))
                        a.then_inc(g_made[s], 1)
                    act.wait_ge(v_product[s], n)
                    act.activation(v[s][:, :, :], two(s, 0), ACT.Copy).then_inc(v_made[s], 1)
                if l == 1:
                    for s in range(s0, s0 + PAIR):
                        act.wait_ge(v1_product[s], use(s, i) + 1)
                        act.activation(v_parts[s][:, :, :, 2, 0:HD],
                                       bank[s][1][:, :].rearrange("p (c h d) -> p c h d", c=C, h=HEADS),
                                       ACT.Copy).then_inc(va_made[s], 1)

            def score(s0, i, l):
                for s in range(s0, s0 + PAIR):
                    act.wait_ge(max_found[s], i * len(ONE_HEAD) + ONE_HEAD.index(l) + 1)
                    for c in range(C):
                        a = act.activation(prob[s][:, c, :], two(s, 1)[:, c, :], ACT.Exp, bias=neg_max[s][:, l, c:c + 1],
                                           accum_out=total[s][:, c:c + 1])
                    a.then_inc(exp_made[s], 1)

            def probs(s0, i, l):
                for s in range(s0, s0 + PAIR):
                    act.wait_ge(turned[s], 2 * (i * LAYERS + l + 1))
                    act.activation(pt[s][:, :, :], two(s, 0), ACT.Copy).then_inc(pt_made[s], 1)

            def round_(s0, i, r):
                if not 1 <= r <= HEADS:
                    return
                h = r - 1
                for s in range(s0, s0 + PAIR):
                    u = use(s, i)
                    act.wait_ge(scored_t[s], FIRST + u * HEADS + h + 1)
                    if h >= 2:
                        act.wait_ge(head_lo[s], u * HEADS + h - 1)
                        act.wait_ge(head_done[s], u * HEADS + h - 1)
                    act.activation(ht_hi[s][:, h % 2], two(s, 1), ACT.Exp)
                    act.activation(ht[s][:, h % 2], two(s, 1), ACT.Exp).then_inc(head_exp[s], 1)

            for s in range(SLOTS):
                act.sem_inc(pt_made[s], FIRST)
            act.wait_ge(weights_ready, 1)
            all_turns(act, turns, {"turn": turn, "project": project, "score": score, "probs": probs, "round": round_})

        @block.vector
        def _(dve):
            for s in range(SLOTS):
                dve.sem_inc(summed[s], FIRST)
            for j in range(PAIR):
                dve.sem_inc(adj_used[j], FIRST)
            dve.memset(unit[:, 0, :], 1.0).then_inc(const_made, 1)
            dve.memset(unit[:, 1, :], 0.0).then_inc(const_made, 1)
            dve.memset(half[:, :], -0.5).then_inc(const_made, 1)
            dve.memset(eps[:, :], EPS).then_inc(const_made, 1)
            for j in range(PAIR):
                dve.memset(v_parts[j][:, :, :, :, HD:HD + 1], 0.0).then_inc(const_made, 1)
            dve.wait_ge(const_made, 4 + PAIR)
            for j in range(PAIR):
                dve.memset(v_parts[j][:, :, :, 2, HD:HD + 1], 1.0).then_inc(const_made, 1)
            dve.wait_ge(cols_in, 16)
            for c in range(C):
                dve.tensor_copy(prob[0][:, c, 0:P], cc("bv1", c).to_broadcast([P, P])).then_inc(spread_made, 1)
            s1, s2 = HD ** -0.5, 128 ** -0.5
            scales = [("bq1", C, s1), ("bqk2", 1, s2), ("bqk3", 1, s2)]
            for name, chunks, scale in scales:
                a = col[:, COLS.index(name), 0:chunks]
                dve.tensor_scalar(a, a, scale, None, ALU.mult)

            step = [0]

            def link(instruction):
                instruction.then_inc(prep_part, 1)
                step[0] += 1
                dve.wait_ge(prep_part, step[0])

            for m, name in enumerate(["qk_0", "vo_0", "qk_4", "vo_4"]):
                dve.wait_ge(prep_product, m + 1)
                a = two(0, 0)
                scale = D ** -0.5 if name.startswith("qk") else 1.0
                link(dve.tensor_scalar(hi_w[name][:, :, :], a, scale, None, ALU.mult))
                dve.scalar_tensor_tensor(lo_w[name][:, :, :], a, scale, hi_w[name][:, :, :].bitcast(F32),
                                         ALU.mult, ALU.subtract).then_inc(prep_read, 1)
                dve.wait_ge(prep_read, m + 1)
                dve.sem_inc(raw_split, 2)
            for n in range(8, STAGED):
                name = RAW[n]
                dve.wait_ge(raw_in[n % 4], 16 * (n // 4 + 1))
                a = stage[n % 4]
                pieces = {"q1": ((0, D, s1),), "qk2": ((0, P, s2), (P, D, 1.0)), "qk3": ((0, P, s2), (P, D, 1.0))}
                for lo, hi, scale in pieces.get(name, ((0, D, 1.0),)):
                    link(dve.tensor_scalar(hi_w[name][:, :, lo:hi], a[:, :, lo:hi], scale, None, ALU.mult))
                    link(dve.scalar_tensor_tensor(lo_w[name][:, :, lo:hi], a[:, :, lo:hi], scale,
                                                  hi_w[name][:, :, lo:hi].bitcast(F32), ALU.mult, ALU.subtract))
                dve.sem_inc(raw_split, 1)
            dve.sem_inc(weights_ready, 1)
            dve.wait_ge(rows_in, 16 * len(ROWS))
            dve.wait_ge(bias_product, 1)
            link(dve.tensor_tensor(row["bo1"], bank[0][1][:, 0:D], row["bo1"], ALU.add))
            link(dve.tensor_tensor(row["b0"][:, :], row["b0"][:, :], row["bo1"], ALU.add))
            link(dve.tensor_tensor(row["b3"][:, :], row["b3"][:, :], row["bo4"], ALU.add))
            dve.sem_inc(rows_ready, 1)
            dve.wait_ge(const_made, 4 + 2 * PAIR)

            def turn(s0, i, l):
                if l != 0:
                    return
                for s in range(s0, s0 + PAIR):
                    u = use(s, i)
                    dve.wait_ge(adj_in[s], (u + 1) * 16)
                    dve.wait_ge(scored[s], FIRST + i * len(ONE_HEAD))
                    dve.tensor_scalar(mask[s][:, :, :], adj_sb[s][:, :, :], 0.0, -BIG, ALU.is_equal,
                                      ALU.mult).then_inc(mask_made[s], 1)
                    dve.wait_ge(mask_made[s], i + 1)
                    dve.sem_inc(adj_used[s], 1)

            def project(s0, i, l):
                for s in range(s0, s0 + PAIR):
                    u = use(s, i)
                    if l == 1:
                        for k, bias in ((0, "bq1"), (2, "bk1")):
                            dve.wait_ge(qk_hi_made[s], 2 * u + 1 + k // 2)
                            for c in range(C):
                                a = dve.scalar_tensor_tensor(parts[s][:, k + 1, c, :], two(s, 1 - k // 2)[:, c, :],
                                                             cc(bias, c), parts[s][:, k, c, :].bitcast(F32),
                                                             ALU.add, ALU.subtract)
                            a.then_inc(qk_lo_made[s], 1)
                    elif l in (0, 4):
                        dve.wait_ge(g_hi_made[s], i * 2 + (1 if l == 0 else 2))
                        dve.tensor_tensor(g_lo[s][:, :, :], two(s, 1), g_hi[s][:, :, :].bitcast(F32),
                                          ALU.subtract).then_inc(g_made[s], 1)
                if l == 1:
                    for s in range(s0, s0 + PAIR):
                        dve.wait_ge(va_made[s], use(s, i) + 1)
                        dve.tensor_tensor(v[s][:, :, :].rearrange("p c (h d) -> p c h d", h=HEADS),
                                          bank[s][1][:, :].rearrange("p (c h d) -> p c h d", c=C, h=HEADS),
                                          v_parts[s][:, :, :, 2, 0:HD], ALU.subtract).then_inc(rest_made[s], 1)

            def score(s0, i, l):
                for s in range(s0, s0 + PAIR):
                    dve.wait_ge(scored[s], FIRST + i * len(ONE_HEAD) + ONE_HEAD.index(l) + 1)
                    dve.tensor_reduce(neg_max[s][:, l, :], two(s, 1), axis=AX.X, op=ALU.max,
                                      negate=True).then_inc(max_found[s], 1)

            def probs(s0, i, l):
                if l == 1:
                    return
                for s in range(s0, s0 + PAIR):
                    n = i * len(ONE_HEAD) + ONE_HEAD.index(l)
                    dve.wait_ge(exp_made[s], n + 1)
                    dve.tensor_scalar(alive1[s][:, :], neg_max[s][:, l, :], 0.5 * BIG, None, ALU.is_lt).then_inc(inv_made[s], 1)
                    dve.reciprocal(inv_total[s][:, :], total[s][:, :]).then_inc(inv_made[s], 1)
                    dve.wait_ge(inv_made[s], 3 * n + 2)
                    factor = alive1[s][:, :] if l in (2, 3) else unit[:, 0, :]
                    dve.tensor_tensor(row_scale[s][:, :], inv_total[s][:, :], factor, ALU.mult).then_inc(inv_made[s], 1)

            def attend(s0, i, l):
                for s in range(s0, s0 + PAIR):
                    n = i * LAYERS + l + 1
                    if l != 1:
                        dve.wait_ge(inv_made[s], 3 * (i * len(ONE_HEAD) + ONE_HEAD.index(l) + 1))
                    dve.wait_ge(attended[s], n)
                    dve.wait_ge(res_made[s], FIRST + i * (LAYERS + 1) + l + 1)
                    if l == 1:
                        a = dve.tensor_tensor(y[s][:, :, :], two(s, 1), xres[s][:, :, :], ALU.add)
                    else:
                        for c in range(C):
                            a = dve.scalar_tensor_tensor(y[s][:, c, :], two(s, 1)[:, c, :], row_scale[s][:, c:c + 1],
                                                         xres[s][:, c, :], ALU.mult, ALU.add)
                    a.then_inc(summed[s], 1)
                    dve.wait_ge(summed[s], FIRST + 2 * n - 1)
                    for c in range(C):
                        a = dve.bn_stats(stats[s][:, c, :], y[s][:, c, :])
                    a.then_inc(summed[s], 1)
                    dve.wait_ge(summed[s], FIRST + 2 * n)
                    dve.memset(wait_cell[s][:, :], 0.0)
                    for c in range(C):
                        a = dve.bn_aggr(mean_var[s][:, c, :], stats[s][:, c, :])
                    a.then_inc(mean_made[s], 1)

            def norm(s0, i, l):
                for s in range(s0, s0 + PAIR):
                    n = i * LAYERS + l + 1
                    dve.wait_ge(mean_made[s], n)
                    dve.wait_ge(rstd_made[s], n)
                    for c in range(C):
                        a = dve.tensor_scalar(y[s][:, c, :], y[s][:, c, :], mean_var[s][:, c, 0:1], rstd[s][:, c:c + 1],
                                              ALU.subtract, ALU.mult)
                    a.then_inc(normed[s], 1)

            def round_(s0, i, r):
                for s in range(s0, s0 + PAIR):
                    u = use(s, i)
                    if r < HEADS:
                        dve.wait_ge(head_scored[s], u * HEADS + r + 1)
                        dve.tensor_reduce(head_max[s][:, r, :], two(s, 0), axis=AX.X, op=ALU.max,
                                          negate=True).then_inc(head_maxed[s], 1)
                for s in range(s0, s0 + PAIR):
                    u = use(s, i)
                    if r < HEADS:
                        dve.wait_ge(head_maxed[s], u * HEADS + r + 1)
                        if r >= 2:
                            dve.wait_ge(scored_t[s], FIRST + u * HEADS + r - 1)
                        for c in range(C):
                            a = dve.tensor_scalar(shifted[s][:, r % 2, c, :], mask[s][:, c, :],
                                                  head_max[s][:, r, c:c + 1], None, ALU.add)
                        a.then_inc(shift_made[s], 1)
                for s in range(s0, s0 + PAIR):
                    u, h = use(s, i), r - 2
                    if r >= 2:
                        dve.wait_ge(head_done[s], u * HEADS + h + 1)
                        src = by_part(s).rearrange("p c (a d) -> p c d a", a=3)
                        dve.tensor_reduce(head_out[s][:, :, head_of(h), :], src, axis=AX.X,
                                          op=ALU.add).then_inc(head_read[s], 1)
                    if r == HEADS:
                        dve.tensor_scalar(alive[s][:, :, :], head_max[s][:, :, :].rearrange("p h c -> p c h"),
                                          0.5 * BIG, None, ALU.is_lt).then_inc(heads_normed[s], 1)
                    if r == HEADS + 1:
                        dve.wait_ge(heads_normed[s], 4 * u + 1)
                        dve.wait_ge(head_read[s], (u + 1) * HEADS)
                        dve.tensor_tensor(den[s][:, :, :], head_out[s][:, :, :, HD], alive[s][:, :, :],
                                          ALU.mult).then_inc(heads_normed[s], 1)
                        dve.wait_ge(heads_normed[s], 4 * u + 2)
                        dve.reciprocal(inv[s][:, :, :], den[s][:, :, :]).then_inc(heads_normed[s], 1)
                        dve.wait_ge(heads_normed[s], 4 * u + 3)
                        for c in range(C):
                            a = dve.tensor_tensor(prob[s][:, c, :].rearrange("p (h d) -> p h d", h=HEADS),
                                                  head_out[s][:, c, :, 0:HD],
                                                  inv[s][:, c, :].unsqueeze(2).to_broadcast([P, HEADS, HD]), ALU.mult)
                        a.then_inc(heads_normed[s], 1)

            all_turns(dve, turns, {"turn": turn, "project": project, "score": score, "probs": probs,
                                   "attend": attend, "norm": norm, "round": round_})

        @block.gpsimd
        def _(pool):
            pool.memset(ident[:, :], 0.0).then_inc(ident_made, 1)
            for j in range(PAIR):
                pool.sem_inc(x_used[j], FIRST)
            for s in range(SLOTS):
                pool.sem_inc(res_made[s], FIRST)
            pool.wait_ge(ident_made, 1)
            pool.affine_select(out=ident[:, :], in_=ident[:, :], compare_op=ALU.not_equal, fill=1.0, base=0,
                               pattern=[[-1, P]], channel_multiplier=1).then_inc(ident_made, 1)
            pool.wait_ge(ident_made, 2)
            pool.tensor_copy(identb[:, :], ident[:, :]).then_inc(ident_made, 1)
            pool.wait_ge(rows_ready, 1)
            pool.wait_ge(const_made, 4)

            def wide(r):
                return row[r][:, :].unsqueeze(1).to_broadcast([P, C, D])

            def residual(s, i, l):
                pool.wait_ge(normed[s], i * LAYERS + l)
                pool.tensor_tensor(xres[s][:, :, :], y[s][:, :, :], wide(f"g{l - 1}"), ALU.mult).then_inc(norm_step[s], 1)
                pool.wait_ge(norm_step[s], 2 * (i * LAYERS + l))
                pool.tensor_tensor(xres[s][:, :, :], xres[s][:, :, :], wide(f"b{l - 1}"), ALU.add).then_inc(res_made[s], 1)

            def turn(s0, i, l):
                for s in range(s0, s0 + PAIR):
                    n = i * LAYERS + l + 1
                    if l == 0:
                        pool.wait_ge(x_in[s], (use(s, i) + 1) * 16)
                        pool.wait_ge(stored[s], (i + 1) * 16)
                        pool.tensor_tensor(xres[s][:, :, :], xin[s][:, :, :], wide("bo0"), ALU.add).then_inc(res_made[s], 1)
                        pool.wait_ge(res_made[s], FIRST + i * (LAYERS + 1) + 1)
                        pool.wait_ge(turned[s], 2 * i * LAYERS + 1)
                        pool.sem_inc(x_used[s], 1)
                    pool.wait_ge(xt_hi_made[s], 2 * n)
                    pool.tensor_tensor(xt_lo[s][:, :, :], xt[s][:, :, :], xt_hi[s][:, :, :].bitcast(F32),
                                       ALU.subtract).then_inc(xt_lo_made[s], 1)
                if l > 0:
                    for s in range(s0, s0 + PAIR):
                        residual(s, i, l)

            def project(s0, i, l):
                if l != 1:
                    return
                for s in range(s0, s0 + PAIR):
                    u = use(s, i)
                    pool.wait_ge(rest_made[s], u + 1)
                    rest = v[s][:, :, :].rearrange("p c (h d) -> p c h d", h=HEADS)
                    ones = unit[:, 0, 0:1].unsqueeze(2).to_broadcast([P, HEADS, HD])
                    for c in range(C):
                        a = pool.tensor_tensor(v_parts[s][:, c, :, 1, 0:HD], rest[:, c], ones, ALU.mult)
                    a.then_inc(vc_made[s], 1)
                    pool.wait_ge(vc_made[s], 2 * u + 1)
                    for c in range(C):
                        a = pool.tensor_tensor(v_parts[s][:, c, :, 0, 0:HD], rest[:, c], v_parts[s][:, c, :, 1, 0:HD],
                                               ALU.subtract)
                    a.then_inc(vc_made[s], 1)

            def round_(s0, i, r):
                if not 1 <= r <= HEADS:
                    return
                h = r - 1
                for s in range(s0, s0 + PAIR):
                    u = use(s, i)
                    pool.wait_ge(head_exp[s], u * HEADS + h + 1)
                    if h >= 2:
                        pool.wait_ge(head_done[s], u * HEADS + h - 1)
                    pool.tensor_tensor(ht_lo[s][:, h % 2], ht[s][:, h % 2], ht_hi[s][:, h % 2],
                                       ALU.subtract).then_inc(head_lo[s], 1)

            def attend(s0, i, l):
                for s in range(s0, s0 + PAIR):
                    n = i * LAYERS + l + 1
                    pool.wait_ge(mean_made[s], n)
                    pool.tensor_tensor(var_eps[s][:, :], mean_var[s][:, :, 1], eps[:, :], ALU.add).then_inc(norm_step[s], 1)
                    pool.wait_ge(norm_step[s], 2 * n - 1)
                    pool.tensor_tensor(rstd[s][:, :], var_eps[s][:, :], half[:, :], ALU.pow).then_inc(rstd_made[s], 1)

            def norm(s0, i, l):
                if l == LAYERS - 1:
                    for s in range(s0, s0 + PAIR):
                        residual(s, i, LAYERS)

            all_turns(pool, turns, {"turn": turn, "project": project, "round": round_, "attend": attend, "norm": norm})


def kernel(x, adj, L0_gnn_Wq, L0_gnn_Wk, L0_gnn_Wv, L0_gnn_Wo, L0_gnn_bo, L0_gnn_gamma, L0_gnn_beta,
           L1_gnn_Wq, L1_gnn_bq, L1_gnn_Wk, L1_gnn_bk, L1_gnn_Wv, L1_gnn_bv, L1_gnn_Wo, L1_gnn_bo, L1_gnn_gamma,
           L1_gnn_beta, L2_gnn_Wq, L2_gnn_bq, L2_gnn_Wk, L2_gnn_bk, L2_gnn_Wc, L2_gnn_ln_g, L2_gnn_ln_b,
           L3_gnn_Wq, L3_gnn_Wk, L3_gnn_Wv, L3_gnn_Wo, L3_gnn_bo, L3_gnn_gamma, L3_gnn_beta):
    import numpy as np
    import concourse.bacc as bacc
    from concourse import mybir as mb
    from concourse.bass_utils import run_bass_kernel_spmd

    a = np.asarray
    qk2 = [np.concatenate([a(L2_gnn_Wq)[k].T, a(L2_gnn_Wk)[k].T], axis=1) for k in range(2)]
    weights = np.stack([a(L0_gnn_Wq).T, a(L0_gnn_Wk).T, a(L0_gnn_Wv).T, a(L0_gnn_Wo),
                        a(L3_gnn_Wq).T, a(L3_gnn_Wk).T, a(L3_gnn_Wv).T, a(L3_gnn_Wo),
                        a(L1_gnn_Wq), a(L1_gnn_Wk), a(L1_gnn_Wv), qk2[0], qk2[1],
                        a(L2_gnn_Wc)[0].T, a(L2_gnn_Wc)[1].T, a(L1_gnn_Wo)])
    g = [a(L0_gnn_gamma), a(L1_gnn_gamma), a(L2_gnn_ln_g)[0], a(L2_gnn_ln_g)[1], a(L3_gnn_gamma)]
    b = [a(L0_gnn_beta), a(L1_gnn_beta), a(L2_gnn_ln_b)[0], a(L2_gnn_ln_b)[1], a(L3_gnn_beta)]
    rows = np.stack(g + b + [a(L0_gnn_bo), a(L1_gnn_bo), a(L3_gnn_bo)])
    rows = np.ascontiguousarray(np.broadcast_to(rows, (128,) + rows.shape))
    bqk2 = [np.concatenate([a(L2_gnn_bq)[k], a(L2_gnn_bk)[k]]) for k in range(2)]
    cols = np.stack(g[:4] + b[:4] + [a(L1_gnn_bq), a(L1_gnn_bk), a(L1_gnn_bv)] + bqk2)
    cols = cols.reshape(len(cols), 2, 128).transpose(2, 0, 1)
    given = {"x": a(x), "adj": a(adj), "weights": weights, "rows": rows, "cols": cols}

    nc = bacc.Bacc("TRN2", target_bir_lowering=False, num_devices=1)
    arrays, args = {}, []
    for name, v in given.items():
        arrays[f"in_{name}"] = v = np.ascontiguousarray(v)
        args.append(nc.dram_tensor(f"in_{name}", v.shape, mb.dt.from_np(v.dtype), kind="ExternalInput").ap())
    args.append(nc.dram_tensor("out_0", given["x"].shape, mb.dt.float32, kind="ExternalOutput").ap())
    graph_stack_kernel(nc, *args)
    return run_bass_kernel_spmd(nc, [arrays], core_ids=[0]).results[0]["out_0"]
```

```python
from contextlib import ExitStack

import concourse.bass as bass
from concourse import mybir

P = 128
N = 256
D = 256
C = N // P
HEADS = 8
HD = D // HEADS
LAYERS = 5
ONE_HEAD = [0, 2, 3, 4]
PAIR = 2
SLOTS = 2 * PAIR
QUARTERS = 4
BIG = 1.0e30
EPS = 1e-5
LO = 32
FIRST = 1

F32 = mybir.dt.float32
F32R = mybir.dt.float32r
F16 = mybir.dt.float16
BF16 = mybir.dt.bfloat16
I32 = mybir.dt.int32
ALU = mybir.AluOpType
ACT = mybir.ActivationFunctionType
AX = mybir.AxisListType

RAW = ["q0T", "k0T", "v0T", "o0", "q3T", "k3T", "v3T", "o3", "q1", "k1", "v1", "qk2", "qk3", "c2", "c3", "o1"]
STAGED = len(RAW) - 1
USED = ["qk_0", "vo_0", "q1", "k1", "v1", "qk2", "c2", "qk3", "c3", "qk_4", "vo_4"]
BETA_OF = {"q1": "b0", "k1": "b0", "v1": "b0", "qk2": "b1", "c2": "b1", "qk3": "b2", "c3": "b2"}
BIAS_OF = {"q1": "bq1", "k1": "bk1", "v1": "bv1", "qk2": "bqk2", "qk3": "bqk3"}
ROWS = ["g0", "g1", "g2", "g3", "g4", "b0", "b1", "b2", "b3", "b4", "bo0", "bo1", "bo4"]
COLS = ["g0", "g1", "g2", "g3", "b0", "b1", "b2", "b3", "bq1", "bk1", "bv1", "bqk2", "bqk3"]

YOUNG, OLD = "young", "old"
ORDER = [
    (YOUNG, 1, "mask", 0), (YOUNG, 0, "turn", 0), (YOUNG, 0, "mask", 0), (YOUNG, 1, "turn", 0), (OLD, 1, "probs", 1),
    (OLD, 0, "probs", 1), (OLD, 1, "attend", 1), (OLD, 0, "attend", 1), (YOUNG, 0, "project", 0),
    (YOUNG, 0, "values", 0), (OLD, 0, "stats", 1), (OLD, 0, "mean", 1), (OLD, 1, "stats", 1), (YOUNG, 0, "score", 0),
    (OLD, 1, "mean", 1), (YOUNG, 0, "split", 0), (OLD, 0, "norm", 1), (OLD, 1, "norm", 1), (YOUNG, 1, "residual", 0),
    (YOUNG, 1, "project", 0), (YOUNG, 0, "inverse", 0), (YOUNG, 1, "values", 0), (OLD, 0, "turn", 2),
    (YOUNG, 0, "residual", 0), (YOUNG, 0, "probs", 0), (OLD, 1, "turn", 2), (YOUNG, 1, "score", 0),
    (YOUNG, 1, "split", 0), (YOUNG, 0, "attend", 0), (YOUNG, 0, "stats", 0), (OLD, 0, "project", 2),
    (YOUNG, 0, "mean", 0), (YOUNG, 1, "probs", 0), (OLD, 1, "residual", 2), (YOUNG, 0, "norm", 0),
    (YOUNG, 1, "inverse", 0), (OLD, 0, "values", 2), (OLD, 0, "score", 2), (OLD, 0, "split", 2),
    (YOUNG, 1, "attend", 0), (OLD, 0, "inverse", 2), (YOUNG, 1, "stats", 0), (OLD, 1, "project", 2),
    (YOUNG, 1, "mean", 0), (YOUNG, 1, "load", 0), (OLD, 0, "residual", 2), (YOUNG, 1, "norm", 0),
    (OLD, 0, "probs", 2), (YOUNG, 0, "turn", 1), (OLD, 1, "values", 2), (OLD, 1, "score", 2), (OLD, 1, "split", 2),
    (OLD, 0, "attend", 2), (OLD, 0, "stats", 2), (YOUNG, 0, "load", 0), (OLD, 0, "mean", 2),
    (YOUNG, 1, "residual", 1), (OLD, 1, "inverse", 2), (YOUNG, 0, "residual", 1), (YOUNG, 1, "turn", 1),
    (YOUNG, 0, "project", 1), (OLD, 1, "probs", 2), (OLD, 0, "norm", 2), (YOUNG, 1, "project", 1),
    (YOUNG, 0, "values", 1), (OLD, 0, "turn", 3), (OLD, 1, "attend", 2), (OLD, 1, "stats", 2), (YOUNG, 0, "stack", 0),
    (OLD, 1, "mean", 2), (YOUNG, 1, "values", 1), (OLD, 0, "residual", 3), (YOUNG, 1, "stack", 0),
    (OLD, 0, "project", 3), (OLD, 1, "norm", 2), (YOUNG, 0, "head_score", 0), (YOUNG, 0, "shift", 0),
    (OLD, 0, "values", 3), (YOUNG, 1, "head_score", 0), (YOUNG, 0, "stack", 1), (YOUNG, 1, "stack", 1),
    (YOUNG, 1, "shift", 0), (OLD, 1, "turn", 3), (YOUNG, 0, "head_score", 1), (YOUNG, 0, "head_exp", 0),
    (YOUNG, 1, "head_score", 1), (OLD, 0, "score", 3), (OLD, 0, "split", 3), (YOUNG, 0, "shift", 1),
    (YOUNG, 0, "head_score", 2), (YOUNG, 1, "shift", 1), (OLD, 1, "project", 3), (YOUNG, 1, "head_score", 2),
    (OLD, 0, "probs", 3), (OLD, 0, "inverse", 3), (OLD, 1, "residual", 3), (YOUNG, 0, "head_exp", 1),
    (YOUNG, 0, "shift", 2), (YOUNG, 0, "head_output", 0), (YOUNG, 0, "stack", 2), (YOUNG, 1, "stack", 2),
    (OLD, 1, "score", 3), (OLD, 0, "attend", 3), (OLD, 0, "stats", 3), (OLD, 1, "inverse", 3),
    (YOUNG, 1, "head_exp", 0), (YOUNG, 0, "head_score", 3), (YOUNG, 1, "stack", 3), (OLD, 0, "mean", 3),
    (YOUNG, 0, "shift", 3), (OLD, 1, "values", 3), (YOUNG, 1, "head_exp", 1), (OLD, 1, "split", 3),
    (YOUNG, 1, "shift", 2), (YOUNG, 1, "head_output", 0), (OLD, 0, "norm", 3), (YOUNG, 0, "head_output", 1),
    (OLD, 1, "probs", 3), (YOUNG, 1, "head_score", 3), (YOUNG, 0, "head_exp", 2), (YOUNG, 0, "head_score", 4),
    (OLD, 0, "turn", 4), (YOUNG, 1, "head_output", 1), (YOUNG, 1, "head_exp", 2), (OLD, 1, "attend", 3),
    (YOUNG, 0, "head_exp", 3), (YOUNG, 0, "stack", 3), (YOUNG, 1, "head_score", 4), (OLD, 1, "stats", 3),
    (YOUNG, 1, "shift", 3), (OLD, 1, "mean", 3), (OLD, 0, "project", 4), (YOUNG, 0, "shift", 4), (OLD, 1, "norm", 3),
    (OLD, 0, "values", 4), (YOUNG, 0, "head_output", 2), (YOUNG, 1, "shift", 4), (OLD, 1, "residual", 4),
    (YOUNG, 1, "head_exp", 3), (YOUNG, 1, "head_output", 2), (OLD, 1, "turn", 4), (YOUNG, 1, "head_score", 5),
    (YOUNG, 0, "head_score", 5), (OLD, 0, "residual", 4), (YOUNG, 0, "head_exp", 4), (OLD, 0, "score", 4),
    (YOUNG, 0, "shift", 5), (YOUNG, 1, "head_exp", 4), (OLD, 0, "split", 4), (YOUNG, 1, "head_output", 3),
    (YOUNG, 0, "head_exp", 5), (YOUNG, 0, "head_output", 3), (YOUNG, 1, "shift", 5), (OLD, 1, "project", 4),
    (OLD, 1, "values", 4), (YOUNG, 1, "head_score", 6), (OLD, 0, "inverse", 4), (YOUNG, 0, "head_score", 6),
    (OLD, 0, "probs", 4), (YOUNG, 0, "shift", 6), (YOUNG, 1, "head_output", 4), (YOUNG, 1, "shift", 6),
    (YOUNG, 1, "head_exp", 5), (OLD, 1, "score", 4), (YOUNG, 0, "head_output", 4), (YOUNG, 1, "head_score", 7),
    (YOUNG, 1, "head_exp", 6), (YOUNG, 0, "head_score", 7), (OLD, 1, "split", 4), (YOUNG, 1, "shift", 7),
    (YOUNG, 0, "shift", 7), (YOUNG, 0, "head_exp", 6), (YOUNG, 1, "head_output", 5), (OLD, 0, "attend", 4),
    (OLD, 1, "probs", 4), (YOUNG, 1, "head_exp", 7), (YOUNG, 0, "head_output", 5), (OLD, 0, "stats", 4),
    (YOUNG, 0, "head_exp", 7), (YOUNG, 0, "head_output", 6), (YOUNG, 1, "head_output", 6), (OLD, 1, "inverse", 4),
    (OLD, 0, "mean", 4), (YOUNG, 1, "head_output", 7), (OLD, 1, "attend", 4), (YOUNG, 0, "head_output", 7),
    (OLD, 1, "stats", 4), (OLD, 1, "mean", 4), (OLD, 0, "norm", 4), (OLD, 0, "residual", 5), (OLD, 1, "norm", 4),
    (OLD, 1, "residual", 5), (OLD, 0, "store", 0), (OLD, 1, "store", 0),
]


def head_of(r):
    return r // 2 + 4 * (r % 2)


def half_turn(steps, young, old):
    for who, seat, step, n in ORDER:
        at = young if who == YOUNG else old
        if at is not None and step in steps:
            steps[step](at[0] * PAIR + seat, at[1], n)


def all_turns(engine, turns, steps):
    half_turn(steps, (0, 0), None)
    with engine.Fori(0, turns - 1) as i:
        half_turn(steps, (1, i), (0, i))
        half_turn(steps, (0, i + 1), (1, i))
    half_turn(steps, (1, turns - 1), (0, turns - 1))
    half_turn(steps, None, (1, turns - 1))


def graph_stack_kernel(nc, x, adj, weights, rows, cols, out):
    graphs = x.shape[0]
    turns = graphs // SLOTS
    with ExitStack() as ctx:
        def sb(name, shape, dt=F32):
            return ctx.enter_context(nc.sbuf_tensor(name, [P] + shape, dt))

        def per_slot(name, shape, dt=F32):
            return [sb(f"{name}{s}", shape, dt) for s in range(SLOTS)]

        def per_seat(name, shape, dt=F32):
            return [sb(f"{name}{j}", shape, dt) for j in range(PAIR)] * 2

        def sem(name):
            return ctx.enter_context(nc.semaphore(name))

        def sems(name):
            return [sem(f"{name}{s}") for s in range(SLOTS)]

        def seat_sems(name):
            return [sem(f"{name}{j}") for j in range(PAIR)] * 2

        ident = sb("ident", [P])
        identb = sb("identb", [P], BF16)
        hi_w = {n: sb(f"wh_{n}", [C, D], F32R) for n in USED}
        lo_w = {n: sb(f"wl_{n}", [C, D], F32R) for n in USED}
        o1 = sb("o1", [C, D])
        row = {n: sb(f"row_{n}", [D]) for n in ROWS if n not in ("bo1", "bo4")}
        col = sb("col", [len(COLS), C])
        v_row = sb("v_row", [2, D], F32R)
        ones = sb("ones", [P], F32R)
        one = sb("one", [1])
        half = sb("half", [C])

        mask = per_slot("mask", [C, N], BF16)
        xres = per_slot("xres", [C, D])
        xt_hi = per_slot("xt_hi", [C, N], F32R)
        xt_lo = per_slot("xt_lo", [C, N], F32R)
        g_hi = per_slot("g_hi", [C, N], F32R)
        g_lo = per_slot("g_lo", [C, N], F32R)
        v_lo = g_hi
        pt_hi, pt_lo = xt_hi, xt_lo
        v = per_slot("v", [C, D], F32R)
        prob = per_slot("prob", [C, N])
        qk = prob
        xt = per_slot("xt", [C, N])
        v_rest = xt
        heads_t = xt
        stage = xt
        y = per_slot("y", [C, D])
        beta_hi = v[0][:, 0, :]
        row["bo1"], row["bo4"] = y[SLOTS - 1][:, 0, :], y[SLOTS - 1][:, 1, :]
        neg_max = per_slot("neg_max", [LAYERS, C])
        total = per_slot("total", [C])
        alive1 = per_slot("alive1", [C])
        inv_total = per_slot("inv_total", [C])
        row_scale = per_slot("row_scale", [C])
        stats = per_slot("stats", [C, 6])
        mean_var = per_slot("mean_var", [C, 2])
        var_eps = per_slot("var_eps", [C])
        rstd = per_slot("rstd", [C])
        wait_cell = per_slot("wait_cell", [1])

        beta_wide = prob[1][:, :, :].rearrange("p c n -> p (c n)")[:, 0:2 * C * (LO + 1)].rearrange("p (l d k) -> p l d k", l=2, d=C)

        xin = per_seat("xin", [C, D])
        adj_sb = per_seat("adj_sb", [C, N], I32)
        parts = per_seat("parts", [4, C, N], F32R)
        stack = per_seat("stack", [2, 2, 2, N], F32R)
        v_parts = per_seat("v_parts", [C, HEADS, 3, HD + 1], BF16)
        shifted = per_seat("shifted", [2, C, N], BF16)
        ht_hi = per_seat("ht_hi", [2, C, N], F16)
        ht_lo = per_seat("ht_lo", [2, C, N], F16)
        ht_odd = per_seat("ht", [C, N])
        ht = [[prob[s], ht_odd[s]] for s in range(SLOTS)]
        head_out = per_seat("head_out", [C, HEADS, HD + 1])
        head_max = per_seat("head_max", [HEADS, C])
        alive = per_seat("alive", [C, HEADS])
        den = per_seat("den", [C, HEADS])
        inv = per_seat("inv", [C, HEADS])

        bank = [[ctx.enter_context(nc.psum_tensor(f"bank{s}{b}", [P, 512], F32)) for b in range(2)]
                for s in range(SLOTS)]

        beta_bank = {"q1": bank[1][0], "k1": bank[2][0], "v1": bank[3][0], "qk2": bank[3][1], "qk3": bank[0][0],
                     "c2": bank[1][1], "c3": bank[2][1]}

        def two(s, b):
            return bank[s][b][:, :].rearrange("p (c n) -> p c n", c=C)

        def by_part(s):
            return bank[s][0][:, 0:C * 3 * (HD + 1)].rearrange("p (c n) -> p c n", c=C)

        cols_in, rows_in, ident_made, o1_in = sem("cols_in"), sem("rows_in"), sem("ident_made"), sem("o1_in")
        raw_in = [sem(f"raw_in{k}") for k in range(4)]
        raw_split, prep_product, prep_part = sem("raw_split"), sem("prep_product"), sem("prep_part")
        prep_read, weights_ready = sem("prep_read"), sem("weights_ready")
        const_made, rows_ready, spread_made, bias_product = sem("const_made"), sem("rows_ready"), sem("spread_made"), sem("bias_product")
        beta_product = sem("beta_product")
        turned, xt_hi_made = sems("turned"), sems("xt_hi_made")
        xt_lo_made = sems("xt_lo_made")
        pt_made, attended = sems("pt_made"), sems("attended")
        g_product, g_hi_made, g_made = sems("g_product"), sems("g_hi_made"), sems("g_made")
        v_product, v_made, pt_lo_made = sems("v_product"), sems("v_made"), sems("pt_lo_made")
        mask_made = sems("mask_made")
        scored, max_found, exp_made = sems("scored"), sems("max_found"), sems("exp_made")
        inv_made = sems("inv_made")
        summed = sems("summed")
        mean_made, rstd_made, normed = sems("mean_made"), sems("rstd_made"), sems("normed")
        scaled = sems("scaled")
        res_made, stored = sems("res_made"), sems("stored")
        x_in, x_used, adj_in, adj_used = seat_sems("x_in"), seat_sems("x_used"), seat_sems("adj_in"), seat_sems("adj_used")
        qk_product, qk_hi_made, qk_lo_made = seat_sems("qk_product"), seat_sems("qk_hi_made"), seat_sems("qk_lo_made")
        v1_product, va_made, rest_made, vc_made = seat_sems("v1_product"), seat_sems("va_made"), seat_sems("rest_made"), seat_sems("vc_made")
        stacked = [[sem(f"stacked{j}_{k}") for k in range(2)] for j in range(PAIR)] * 2
        head_scored, head_maxed, shift_made = seat_sems("head_scored"), seat_sems("head_maxed"), seat_sems("shift_made")
        scored_t, head_exp, head_lo = seat_sems("scored_t"), seat_sems("head_exp"), seat_sems("head_lo")
        head_done, head_read = seat_sems("head_done"), seat_sems("head_read")
        heads_normed = seat_sems("heads_normed")

        block = ctx.enter_context(nc.Block())

        def cc(name, c):
            return col[:, COLS.index(name), c:c + 1]

        def use(s, i):
            return i * 2 + s // PAIR

        @block.sync
        def _(sp):
            for s in range(SLOTS):
                sp.sem_inc(stored[s], 16)
            sp.dma_start(col[:, :, :], cols).then_inc(cols_in, 16)

            def load(s, i):
                u = use(s, i)
                sp.wait_ge(x_used[s], FIRST + u)
                sp.dma_start(xin[s][:, :, :], x[i * SLOTS + s].rearrange("(c p) d -> p c d", p=P)).then_inc(x_in[s], 16)
                sp.wait_ge(adj_used[s], FIRST + u)
                sp.dma_start(adj_sb[s][:, :, :], adj[i * SLOTS + s].rearrange("(c p) d -> p c d", p=P)).then_inc(adj_in[s], 16)

            for n in range(STAGED):
                if n >= 4:
                    sp.wait_ge(raw_split, n - 3)
                sp.dma_start(stage[n % 4][:, :, :], weights[n].rearrange("(c p) n -> p c n", p=P)).then_inc(raw_in[n % 4], 16)
                if n == 3:
                    sp.dma_start(o1[:, :, :], weights[STAGED].rearrange("(c p) n -> p c n", p=P)).then_inc(o1_in, 16)
                    for s in range(PAIR):
                        load(s, 0)
            for m, r in enumerate(ROWS):
                sp.dma_start(row[r] if r in ("bo1", "bo4") else row[r][:, :], rows[:, m, :]).then_inc(rows_in, 16)

            def stack_quarter(s, i, q):
                u = use(s, i)
                if q == 0:
                    sp.wait_ge(qk_lo_made[s], 2 * u + 2)
                sp.wait_ge(scored_t[s], FIRST + u * HEADS + (2 * (q - 1) if q >= 2 else 0))
                for part, (first, step) in enumerate(((0, 2), (0, 3), (1, 1), (1, 2))):
                    sp.dma_start(stack[s][32 * part:32 * part + 32, q % 2].bitcast(F32),
                                 parts[s][32 * q:32 * q + 32, first:first + step + 1:step].bitcast(F32)
                                 ).then_inc(stacked[s][q % 2], 16)

            def load_next(s, i, _):
                if s < PAIR:
                    load(s + PAIR, i)
                elif not (isinstance(i, int) and i + 1 == turns):
                    load(s - PAIR, i + 1)

            def store(s, i, _):
                sp.wait_ge(res_made[s], FIRST + (i + 1) * (LAYERS + 1))
                sp.dma_start(out[i * SLOTS + s].rearrange("(c p) d -> p c d", p=P), xres[s][:, :, :]).then_inc(stored[s], 16)

            all_turns(sp, turns, {"stack": stack_quarter, "load": load_next, "store": store})
            for s in range(SLOTS):
                sp.wait_ge(stored[s], 16 * (turns + 1))

        @block.tensor
        def _(pe):
            for s in range(SLOTS):
                pe.sem_inc(scored[s], FIRST)
            for j in range(PAIR):
                pe.sem_inc(scored_t[j], FIRST)
            for m in range(4):
                a, b = (2 * m) % 4, (2 * m + 1) % 4
                pe.wait_ge(raw_in[a], 16 * (m // 2 + 1))
                pe.wait_ge(raw_in[b], 16 * (m // 2 + 1))
                if m:
                    pe.wait_ge(prep_read, m)
                for c in range(C):
                    for e in range(C):
                        mm = pe.matmul(two(0, 0)[:, c, :], stage[a][:, e, c * P:(c + 1) * P], stage[b][:, e, :],
                                       start=(e == 0), stop=(e == C - 1))
                mm.then_inc(prep_product, 1)
            pe.wait_ge(cols_in, 16)
            pe.wait_ge(spread_made, 1)
            for n in range(8, STAGED):
                a = stage[n % 4]
                pe.wait_ge(raw_in[n % 4], 16 * (n // 4 + 1))
                if RAW[n] in ("c2", "c3"):
                    for d in range(C):
                        mm = pe.matmul(beta_bank[RAW[n]][0:LO + 1, 0:D],
                                       beta_wide[:, int(RAW[n][1]) - 2, d, :], a[:, d, :], start=(d == 0), stop=(d == C - 1))
                else:
                    for e in range(C):
                        for d in range(C):
                            mm = pe.matmul(beta_bank[RAW[n]][:, e:e + 1], a[:, d, e * P:(e + 1) * P],
                                           cc(BETA_OF[RAW[n]], d), start=(d == 0), stop=(d == C - 1))
                mm.then_inc(beta_product, 1)
            pe.wait_ge(spread_made, 3)
            pe.wait_ge(o1_in, 16)
            for e in range(C):
                mm = pe.matmul(bank[0][1][:, 0:D], prob[0][:, e, 0:P], o1[:, e, :], start=(e == 0), stop=(e == C - 1))
            mm.then_inc(bias_product, 1)
            pe.wait_ge(ident_made, 3)
            pe.wait_ge(weights_ready, 1)
            pe.wait_ge(rows_ready, 1)

            def three(dst, l_hi, l_lo, r_hi, r_lo, first, last):
                pe.matmul(dst, l_hi, r_hi, start=first, stop=False)
                pe.matmul(dst, l_hi, r_lo, start=False, stop=False)
                return pe.matmul(dst, l_lo, r_hi, start=False, stop=last)

            def transposed_product(s, b, weight):
                dst, h, w = two(s, b), hi_w[weight], lo_w[weight]
                for c in range(C):
                    for d in range(C):
                        k = slice(c * P, (c + 1) * P)
                        mm = three(dst[:, c, :], h[:, d, k], w[:, d, k], xt_hi[s][:, d, :], xt_lo[s][:, d, :],
                                   d == 0, d == C - 1)
                return mm

            def product(s, b, weight, added=None):
                dst, h, w = two(s, b), hi_w[weight], lo_w[weight]
                for c in range(C):
                    for d in range(C):
                        k = slice(c * P, (c + 1) * P)
                        mm = three(dst[:, c, :], xt_hi[s][:, d, k], xt_lo[s][:, d, k], h[:, d, :], w[:, d, :],
                                   d == 0, added is None and d == C - 1)
                    if added is not None:
                        mm = pe.matmul(dst[:, c, :], ones[0:LO + 1, :], v_row[0:LO + 1, added, :], start=False, stop=True)
                return mm

            def turn(s, i, l):
                dst = two(s, 0)
                if l == 0:
                    pe.wait_ge(x_in[s], (use(s, i) + 1) * 16)
                    pe.wait_ge(pt_made[s], FIRST + i * LAYERS)
                else:
                    pe.wait_ge(normed[s], i * LAYERS + l)
                src = xin[s] if l == 0 else y[s]
                for c in range(C):
                    for d in range(C):
                        mm = pe.transpose(dst[:, d, c * P:(c + 1) * P], src[:, c, d * P:(d + 1) * P], ident[:, :])
                mm.then_inc(turned[s], 1)

            def project(s, i, l):
                pe.wait_ge(xt_hi_made[s], i * LAYERS + l + 1)
                pe.wait_ge(xt_lo_made[s], i * (LAYERS + 1) + (l + 1 if l < LAYERS - 1 else LAYERS + 1))
                if l == 0:
                    pe.wait_ge(summed[s], FIRST + i * 2 * LAYERS)
                if l == 1:
                    transposed_product(s, 1, "q1").then_inc(qk_product[s], 1)
                    transposed_product(s, 0, "k1").then_inc(qk_product[s], 1)
                else:
                    transposed_product(s, 1, {0: "qk_0", 2: "qk2", 3: "qk3", 4: "qk_4"}[l]).then_inc(g_product[s], 1)

            def values(s, i, l):
                if l == 1:
                    pe.wait_ge(qk_lo_made[s], 2 * use(s, i) + 1)
                    product(s, 1, "v1").then_inc(v1_product[s], 1)
                else:
                    product(s, 0, {0: "vo_0", 2: "c2", 3: "c3", 4: "vo_4"}[l],
                            l - 2 if l in (2, 3) else None).then_inc(v_product[s], 1)

            def score(s, i, l):
                dst = two(s, 1)
                pe.wait_ge(g_made[s], i * len(ONE_HEAD) + ONE_HEAD.index(l) + 1)
                if l == 0:
                    pe.wait_ge(mask_made[s], i + 1)
                for c in range(C):
                    k = slice(c * P, (c + 1) * P)
                    pe.matmul(dst[:, c, :], identb[:, :], mask[s][:, c, :], start=True, stop=False)
                    if l in (0, 4):
                        for e in range(C):
                            mm = three(dst[:, c, :], g_hi[s][:, e, k], g_lo[s][:, e, k], xt_hi[s][:, e, :],
                                       xt_lo[s][:, e, :], False, e == C - 1)
                    else:
                        mm = pe.matmul(dst[:, c, :], qk[s][:, 0, k], qk[s][:, 1, :], start=False, stop=True)
                mm.then_inc(scored[s], 1)

            def probs(s, i, l):
                dst = two(s, 0)
                if l == 1:
                    pe.wait_ge(heads_normed[s], 8 * use(s, i) + 8)
                else:
                    a = i * len(ONE_HEAD) + ONE_HEAD.index(l) + 1
                    pe.wait_ge(v_made[s], 2 * a)
                    pe.wait_ge(exp_made[s], a)
                for c in range(C):
                    for k in range(C):
                        src = y[s] if l == 1 else prob[s]
                        mm = pe.transpose(dst[:, k, c * P:(c + 1) * P], src[:, c, k * P:(k + 1) * P], ident[:, :])
                mm.then_inc(turned[s], 1)

            def attend(s, i, l):
                dst = two(s, 1)
                pe.wait_ge(pt_made[s], FIRST + i * LAYERS + l + 1)
                if l != 1:
                    pe.wait_ge(pt_lo_made[s], i * len(ONE_HEAD) + ONE_HEAD.index(l) + 1)
                for c in range(C):
                    for k in range(C):
                        q = slice(c * P, (c + 1) * P)
                        if l == 1:
                            mm = pe.matmul(dst[:, c, :], heads_t[s][:, k, q], o1[:, k, :], start=(k == 0), stop=(k == C - 1))
                        else:
                            mm = three(dst[:, c, :], pt_hi[s][:, k, q], pt_lo[s][:, k, q],
                                       v[s][:, k, :], v_lo[s][:, k, :], k == 0, k == C - 1)
                mm.then_inc(attended[s], 1)

            def head_score(s, i, r):
                u, dst, q = use(s, i), two(s, 0), r // 2
                if r % 2 == 0:
                    pe.wait_ge(stacked[s][q % 2], u * 128 + 64 * (q // 2) + 64)
                if r == 1 or r == 2:
                    pe.wait_ge(head_maxed[s], u * HEADS + r)
                if r >= 3:
                    pe.wait_ge(head_read[s], u * HEADS + r - 2)
                for c in range(C):
                    pe.matmul(dst[:, c, :], identb[:, :], mask[s][:, c, :], start=True, stop=False)
                    mm = pe.matmul(dst[:, c, :], stack[s][:, q % 2, 0, r % 2, c * P:(c + 1) * P],
                                   stack[s][:, q % 2, 1, r % 2, :], start=False, stop=True)
                mm.then_inc(head_scored[s], 1)

            def head_exp_t(s, i, r):
                u, dst, q = use(s, i), two(s, 1), r // 2
                pe.wait_ge(shift_made[s], u * HEADS + r + 1)
                if r == 0:
                    pe.wait_ge(rest_made[s], u + 1)
                else:
                    pe.wait_ge(head_exp[s], u * HEADS + r)
                for k in range(C):
                    kk = slice(k * P, (k + 1) * P)
                    pe.matmul(dst[:, k, :], stack[s][:, q % 2, 1, r % 2, kk], stack[s][:, q % 2, 0, r % 2, :],
                              start=True, stop=False)
                    for c in range(C):
                        mm = pe.matmul(dst[:, k, c * P:(c + 1) * P], shifted[s][:, r % 2, c, kk], identb[:, :],
                                       start=False, stop=(c == C - 1))
                mm.then_inc(scored_t[s], 1)

            def head_output(s, i, r):
                u, dst = use(s, i), by_part(s)
                pe.wait_ge(head_lo[s], u * HEADS + r + 1)
                if r == 0:
                    pe.wait_ge(vc_made[s], 2 * u + 2)
                if r + 2 < HEADS:
                    pe.wait_ge(head_maxed[s], u * HEADS + r + 3)
                else:
                    pe.wait_ge(head_read[s], u * HEADS + r)
                for c in range(C):
                    for k in range(C):
                        q = slice(c * P, (c + 1) * P)
                        right = v_parts[s][:, k, head_of(r)].rearrange("p a d -> p (a d)")
                        pe.matmul(dst[:, c, :], ht_hi[s][:, r % 2, k, q], right, start=(k == 0), stop=False)
                        mm = pe.matmul(dst[:, c, HD + 1:], ht_lo[s][:, r % 2, k, q], right[:, HD + 1:],
                                       start=False, stop=(k == C - 1))
                mm.then_inc(head_done[s], 1)

            all_turns(pe, turns, {"turn": turn, "project": project, "values": values, "score": score, "probs": probs,
                                  "attend": attend, "head_score": head_score, "head_exp": head_exp_t,
                                  "head_output": head_output})

        @block.scalar
        def _(act):
            def turn(s, i, l):
                if l < LAYERS - 1:
                    act.wait_ge(turned[s], 2 * (i * LAYERS + l) + 1)
                    act.activation(xt_hi[s][:, :, :], two(s, 0), ACT.Copy).then_inc(xt_hi_made[s], 1)
                else:
                    act.wait_ge(xt_lo_made[s], i * (LAYERS + 1) + LAYERS)
                    act.activation(xt_hi[s][:, :, :], xt[s][:, :, :], ACT.Copy).then_inc(xt_hi_made[s], 1)

            def project(s, i, l):
                u = use(s, i)
                n = i * len(ONE_HEAD) + (ONE_HEAD.index(l) + 1 if l != 1 else 0)
                if l == 1:
                    for k, bias in ((0, "bq1"), (2, "bk1")):
                        act.wait_ge(qk_product[s], 2 * u + 1 + k // 2)
                        for c in range(C):
                            a = act.activation(parts[s][:, k, c, :], two(s, 1 - k // 2)[:, c, :], ACT.Identity,
                                               bias=cc(bias, c))
                        a.then_inc(qk_hi_made[s], 1)
                    return
                act.wait_ge(g_product[s], n)
                if l in (0, 4):
                    act.activation(g_hi[s][:, :, :], two(s, 1), ACT.Copy).then_inc(g_hi_made[s], 1)
                else:
                    for c in range(C):
                        a = act.activation(qk[s][:, c, :], two(s, 1)[:, c, :], ACT.Identity, bias=cc(f"bqk{l}", c))
                    a.then_inc(g_made[s], 1)

            def values(s, i, l):
                if l == 1:
                    act.wait_ge(v1_product[s], use(s, i) + 1)
                    act.activation(v_parts[s][:, :, :, 2, 0:HD],
                                   bank[s][1][:, :].rearrange("p (c h d) -> p c h d", c=C, h=HEADS),
                                   ACT.Copy).then_inc(va_made[s], 1)
                else:
                    act.wait_ge(v_product[s], i * len(ONE_HEAD) + ONE_HEAD.index(l) + 1)
                    act.activation(v[s][:, :, :], two(s, 0), ACT.Copy).then_inc(v_made[s], 1)

            def score(s, i, l):
                act.wait_ge(max_found[s], i * len(ONE_HEAD) + ONE_HEAD.index(l) + 1)
                for c in range(C):
                    a = act.activation(prob[s][:, c, :], two(s, 1)[:, c, :], ACT.Exp, bias=neg_max[s][:, l, c:c + 1],
                                       accum_out=total[s][:, c:c + 1])
                a.then_inc(exp_made[s], 1)

            def probs(s, i, l):
                act.wait_ge(turned[s], 2 * (i * LAYERS + l + 1))
                dst = heads_t if l == 1 else pt_hi
                act.activation(dst[s][:, :, :], two(s, 0), ACT.Copy).then_inc(pt_made[s], 1)

            def head_exp_t(s, i, r):
                u = use(s, i)
                act.wait_ge(scored_t[s], FIRST + u * HEADS + r + 1)
                if r >= 2:
                    act.wait_ge(head_lo[s], u * HEADS + r - 1)
                    act.wait_ge(head_done[s], u * HEADS + r - 1)
                act.activation(ht_hi[s][:, r % 2], two(s, 1), ACT.Exp)
                act.activation(ht[s][r % 2][:, :, :], two(s, 1), ACT.Exp).then_inc(head_exp[s], 1)

            for s in range(SLOTS):
                act.sem_inc(pt_made[s], FIRST)
            act.wait_ge(weights_ready, 1)
            all_turns(act, turns, {"turn": turn, "project": project, "values": values, "score": score, "probs": probs,
                                   "head_exp": head_exp_t})

        @block.vector
        def _(dve):
            for s in range(SLOTS):
                dve.sem_inc(summed[s], FIRST)
            for j in range(PAIR):
                dve.sem_inc(adj_used[j], FIRST)
            dve.memset(one[:, :], 1.0).then_inc(const_made, 1)
            dve.memset(half[:, :], -0.5).then_inc(const_made, 1)
            for j in range(PAIR):
                dve.memset(v_parts[j][:, :, :, :, HD:HD + 1], 0.0).then_inc(const_made, 1)
            dve.wait_ge(const_made, 2 + PAIR)
            for j in range(PAIR):
                dve.memset(v_parts[j][:, :, :, 2, HD:HD + 1], 1.0).then_inc(const_made, 1)
            dve.tensor_copy(ones[:, :], one[:, 0:1].to_broadcast([P, P])).then_inc(const_made, 1)
            dve.tensor_scalar(v_row[:, :, :].rearrange("p l d -> p (l d)"), one[:, 0:1].to_broadcast([P, 2 * D]), 0.0, None,
                              ALU.mult).then_inc(const_made, 1)
            dve.wait_ge(cols_in, 16)
            for l in range(2):
                for d in range(C):
                    a = dve.tensor_copy(beta_wide[:, l, d, :], cc(f"b{l + 1}", d).to_broadcast([P, LO + 1]))
            a.then_inc(spread_made, 1)
            s1, s2 = HD ** -0.5, 128 ** -0.5
            step = [0]

            def link(instruction):
                instruction.then_inc(prep_part, 1)
                step[0] += 1
                dve.wait_ge(prep_part, step[0])

            for m, name in enumerate(["qk_0", "vo_0", "qk_4", "vo_4"]):
                dve.wait_ge(prep_product, m + 1)
                a = two(0, 0)
                scale = D ** -0.5 if name.startswith("qk") else 1.0
                link(dve.tensor_scalar(hi_w[name][:, :, :], a, scale, None, ALU.mult))
                dve.scalar_tensor_tensor(lo_w[name][:, :, :], a, scale, hi_w[name][:, :, :].bitcast(F32),
                                         ALU.mult, ALU.subtract).then_inc(prep_read, 1)
                dve.wait_ge(prep_read, m + 1)
                dve.sem_inc(raw_split, 2)
            for n in range(8, STAGED):
                name, a, beta = RAW[n], stage[n % 4], BETA_OF[RAW[n]]
                dve.wait_ge(raw_in[n % 4], 16 * (n // 4 + 1))
                dve.wait_ge(beta_product, n - 7)
                pieces = {"q1": ((0, D, s1),), "qk2": ((0, P, s2), (P, D, 1.0)), "qk3": ((0, P, s2), (P, D, 1.0))}
                for lo, hi, scale in pieces.get(name, ((0, D, 1.0),)):
                    for c in range(C):
                        m = dve.tensor_scalar(a[:, c, lo:hi], a[:, c, lo:hi], cc("g" + beta[1], c), scale, ALU.mult, ALU.mult)
                link(m)
                link(dve.tensor_copy(hi_w[name][:, :, :], a[:, :, :]))
                dve.tensor_tensor(lo_w[name][:, :, :], a[:, :, :], hi_w[name][:, :, :].bitcast(F32), ALU.subtract)
                if name in ("c2", "c3"):
                    l = int(name[1]) - 2
                    src = beta_bank[name]
                    link(dve.tensor_copy(beta_hi[0:LO + 1, :], src[0:LO + 1, 0:D]))
                    if l == 0:
                        dve.wait_ge(const_made, 4 + 2 * PAIR)
                    dve.tensor_copy(v_row[0:1, l, :], beta_hi[0:1, :].bitcast(F32))
                    link(dve.tensor_tensor(v_row[LO:LO + 1, l, :], src[LO:LO + 1, 0:D], beta_hi[LO:LO + 1, :].bitcast(F32),
                                           ALU.subtract))
                else:
                    bias = col[:, COLS.index(BIAS_OF[name]), :]
                    link(dve.tensor_tensor(bias, beta_bank[name][:, 0:C], bias, ALU.add))
                    if name != "v1" and name != "k1":
                        chunks, scale = (C, s1) if name == "q1" else (1, s2)
                        link(dve.tensor_scalar(bias[:, 0:chunks], bias[:, 0:chunks], scale, None, ALU.mult))
                    if name == "v1":
                        for c in range(C):
                            dve.tensor_copy(prob[0][:, c, 0:P], cc("bv1", c).to_broadcast([P, P])).then_inc(spread_made, 1)
                dve.sem_inc(raw_split, 1)
            dve.sem_inc(weights_ready, 1)
            dve.wait_ge(rows_in, 16 * len(ROWS))
            dve.wait_ge(bias_product, 1)
            link(dve.tensor_tensor(row["bo1"], bank[0][1][:, 0:D], row["bo1"], ALU.add))
            link(dve.tensor_tensor(row["b0"][:, :], row["b0"][:, :], row["bo1"], ALU.add))
            link(dve.tensor_tensor(row["b3"][:, :], row["b3"][:, :], row["bo4"], ALU.add))
            dve.sem_inc(rows_ready, 1)
            dve.wait_ge(const_made, 4 + 2 * PAIR)

            def turn(s, i, l):
                n = i * LAYERS + l + 1
                src = two(s, 0)
                if l == LAYERS - 1:
                    dve.wait_ge(turned[s], 2 * n - 1)
                    for c in range(C):
                        a = dve.tensor_scalar(xt[s][:, c, :], two(s, 0)[:, c, :], cc(f"g{l - 1}", c), cc(f"b{l - 1}", c),
                                              ALU.mult, ALU.add)
                    a.then_inc(xt_lo_made[s], 1)
                    src = xt[s][:, :, :]
                dve.wait_ge(xt_hi_made[s], n)
                dve.tensor_tensor(xt_lo[s][:, :, :], src, xt_hi[s][:, :, :].bitcast(F32),
                                  ALU.subtract).then_inc(xt_lo_made[s], 1)

            def make_mask(s, i, _):
                u = use(s, i)
                dve.wait_ge(adj_in[s], (u + 1) * 16)
                dve.wait_ge(scored[s], FIRST + i * len(ONE_HEAD))
                dve.tensor_scalar(mask[s][:, :, :], adj_sb[s][:, :, :], 0.0, -BIG, ALU.is_equal,
                                  ALU.mult).then_inc(mask_made[s], 1)
                dve.wait_ge(mask_made[s], i + 1)
                dve.sem_inc(adj_used[s], 1)

            def project(s, i, l):
                u = use(s, i)
                if l == 1:
                    for k, bias in ((0, "bq1"), (2, "bk1")):
                        dve.wait_ge(qk_hi_made[s], 2 * u + 1 + k // 2)
                        for c in range(C):
                            a = dve.scalar_tensor_tensor(parts[s][:, k + 1, c, :], two(s, 1 - k // 2)[:, c, :],
                                                         cc(bias, c), parts[s][:, k, c, :].bitcast(F32),
                                                         ALU.add, ALU.subtract)
                        a.then_inc(qk_lo_made[s], 1)
                elif l in (0, 4):
                    dve.wait_ge(g_hi_made[s], i * 2 + (1 if l == 0 else 2))
                    dve.tensor_tensor(g_lo[s][:, :, :], two(s, 1), g_hi[s][:, :, :].bitcast(F32),
                                      ALU.subtract).then_inc(g_made[s], 1)

            def values(s, i, l):
                if l == 1:
                    dve.wait_ge(va_made[s], use(s, i) + 1)
                    dve.tensor_tensor(v_rest[s][:, :, :].rearrange("p c (h d) -> p c h d", h=HEADS),
                                      bank[s][1][:, :].rearrange("p (c h d) -> p c h d", c=C, h=HEADS),
                                      v_parts[s][:, :, :, 2, 0:HD], ALU.subtract).then_inc(rest_made[s], 1)

            def score(s, i, l):
                dve.wait_ge(scored[s], FIRST + i * len(ONE_HEAD) + ONE_HEAD.index(l) + 1)
                dve.tensor_reduce(neg_max[s][:, l, :], two(s, 1), axis=AX.X, op=ALU.max,
                                  negate=True).then_inc(max_found[s], 1)

            def split(s, i, l):
                n = i * len(ONE_HEAD) + ONE_HEAD.index(l)
                dve.wait_ge(scored[s], FIRST + n + 1)
                dve.wait_ge(v_made[s], 2 * n + 1)
                dve.tensor_tensor(v_lo[s][:, :, :], two(s, 0), v[s][:, :, :].bitcast(F32), ALU.subtract).then_inc(v_made[s], 1)

            def probs(s, i, l):
                if l == 1:
                    return
                dve.wait_ge(pt_made[s], FIRST + i * LAYERS + l + 1)
                dve.tensor_tensor(pt_lo[s][:, :, :], two(s, 0), pt_hi[s][:, :, :].bitcast(F32), ALU.subtract).then_inc(pt_lo_made[s], 1)

            def inverse(s, i, l):
                n = i * len(ONE_HEAD) + ONE_HEAD.index(l)
                dve.wait_ge(exp_made[s], n + 1)
                dve.tensor_scalar(alive1[s][:, :], neg_max[s][:, l, :], 0.5 * BIG, None, ALU.is_lt).then_inc(inv_made[s], 1)
                dve.reciprocal(inv_total[s][:, :], total[s][:, :]).then_inc(inv_made[s], 1)
                dve.wait_ge(inv_made[s], 3 * n + 2)
                factor = alive1[s][:, :] if l in (2, 3) else one[:, 0:1].to_broadcast([P, C])
                dve.tensor_tensor(row_scale[s][:, :], inv_total[s][:, :], factor, ALU.mult).then_inc(inv_made[s], 1)

            def attend(s, i, l):
                n = i * LAYERS + l + 1
                if l != 1:
                    dve.wait_ge(inv_made[s], 3 * (i * len(ONE_HEAD) + ONE_HEAD.index(l) + 1))
                dve.wait_ge(attended[s], n)
                dve.wait_ge(res_made[s], FIRST + i * (LAYERS + 1) + l + 1)
                if l == 1:
                    a = dve.tensor_tensor(y[s][:, :, :], two(s, 1), xres[s][:, :, :], ALU.add)
                else:
                    for c in range(C):
                        a = dve.scalar_tensor_tensor(y[s][:, c, :], two(s, 1)[:, c, :], row_scale[s][:, c:c + 1],
                                                     xres[s][:, c, :], ALU.mult, ALU.add)
                a.then_inc(summed[s], 1)

            def row_stats(s, i, l):
                n = i * LAYERS + l + 1
                dve.wait_ge(summed[s], FIRST + 2 * n - 1)
                for c in range(C):
                    a = dve.bn_stats(stats[s][:, c, :], y[s][:, c, :])
                a.then_inc(summed[s], 1)

            def mean(s, i, l):
                n = i * LAYERS + l + 1
                dve.wait_ge(summed[s], FIRST + 2 * n)
                dve.memset(wait_cell[s][:, :], 0.0)
                for c in range(C):
                    a = dve.bn_aggr(mean_var[s][:, c, :], stats[s][:, c, :])
                a.then_inc(mean_made[s], 1)
                dve.wait_ge(mean_made[s], 2 * n - 1)
                dve.tensor_scalar(var_eps[s][:, :], mean_var[s][:, :, 1], EPS, None, ALU.add).then_inc(mean_made[s], 1)

            def norm(s, i, l):
                n = i * LAYERS + l + 1
                dve.wait_ge(rstd_made[s], n)
                for c in range(C):
                    a = dve.tensor_scalar(y[s][:, c, :], y[s][:, c, :], mean_var[s][:, c, 0:1], rstd[s][:, c:c + 1],
                                          ALU.subtract, ALU.mult)
                a.then_inc(normed[s], 1)

            def head_score(s, i, r):
                u = use(s, i)
                dve.wait_ge(head_scored[s], u * HEADS + r + 1)
                dve.tensor_reduce(head_max[s][:, r, :], two(s, 0), axis=AX.X, op=ALU.max,
                                  negate=True).then_inc(head_maxed[s], 1)

            def shift(s, i, r):
                u = use(s, i)
                dve.wait_ge(head_maxed[s], u * HEADS + r + 1)
                if r >= 2:
                    dve.wait_ge(scored_t[s], FIRST + u * HEADS + r - 1)
                for c in range(C):
                    a = dve.tensor_scalar(shifted[s][:, r % 2, c, :], mask[s][:, c, :], head_max[s][:, r, c:c + 1],
                                          None, ALU.add)
                a.then_inc(shift_made[s], 1)

            def head_output(s, i, r):
                dve.wait_ge(head_done[s], use(s, i) * HEADS + r + 1)
                src = by_part(s).rearrange("p c (a d) -> p c d a", a=3)
                dve.tensor_reduce(head_out[s][:, :, head_of(r), :], src, axis=AX.X, op=ALU.add).then_inc(head_read[s], 1)
                if r % 4 == 3:
                    normed_heads(s, i, r // 4)

            def normed_heads(s, i, part):
                n = 2 * use(s, i) + part
                k = slice(4 * part, 4 * part + 4)
                heads = head_out[s][:, :, :, :].rearrange("p c (b q) d -> p c b q d", b=2)[:, :, :, 2 * part:2 * part + 2, :]
                dve.tensor_scalar(alive[s][:, :, k], head_max[s][:, k, :].rearrange("p h c -> p c h"),
                                  0.5 * BIG, None, ALU.is_lt).then_inc(heads_normed[s], 1)
                dve.wait_ge(heads_normed[s], 4 * n + 1)
                dve.wait_ge(head_read[s], (n + 1) * QUARTERS)
                for c in range(C):
                    a = dve.tensor_tensor(den[s][:, c, k].rearrange("p (b q) -> p b q", b=2), heads[:, c, :, :, HD],
                                          alive[s][:, c, k].rearrange("p (b q) -> p b q", b=2), ALU.mult)
                a.then_inc(heads_normed[s], 1)
                dve.wait_ge(heads_normed[s], 4 * n + 2)
                dve.reciprocal(inv[s][:, :, k], den[s][:, :, k]).then_inc(heads_normed[s], 1)
                dve.wait_ge(heads_normed[s], 4 * n + 3)
                if part == 0:
                    dve.wait_ge(res_made[s], FIRST + i * (LAYERS + 1) + 2)
                for c in range(C):
                    factor = inv[s][:, c, k].rearrange("p (b q) -> p b q", b=2).unsqueeze(3).to_broadcast([P, 2, 2, HD])
                    y_heads = y[s][:, c, :].rearrange("p (b q d) -> p b q d", b=2, q=QUARTERS)[:, :, 2 * part:2 * part + 2, :]
                    a = dve.tensor_tensor(y_heads, heads[:, c, :, :, 0:HD], factor, ALU.mult)
                a.then_inc(heads_normed[s], 1)

            all_turns(dve, turns, {"turn": turn, "mask": make_mask, "project": project, "values": values, "score": score,
                                   "split": split, "probs": probs, "inverse": inverse, "attend": attend, "stats": row_stats, "mean": mean, "norm": norm,
                                   "head_score": head_score, "shift": shift, "head_output": head_output})

        @block.gpsimd
        def _(pool):
            pool.memset(ident[:, :], 0.0).then_inc(ident_made, 1)
            for j in range(PAIR):
                pool.sem_inc(x_used[j], FIRST)
            for s in range(SLOTS):
                pool.sem_inc(res_made[s], FIRST)
            pool.wait_ge(ident_made, 1)
            pool.affine_select(out=ident[:, :], in_=ident[:, :], compare_op=ALU.not_equal, fill=1.0, base=0,
                               pattern=[[-1, P]], channel_multiplier=1).then_inc(ident_made, 1)
            pool.wait_ge(ident_made, 2)
            pool.tensor_copy(identb[:, :], ident[:, :]).then_inc(ident_made, 1)
            pool.wait_ge(rows_ready, 1)
            pool.wait_ge(const_made, 2)

            def wide(r):
                return row[r][:, :].unsqueeze(1).to_broadcast([P, C, D])

            def residual(s, i, l):
                if l == 0:
                    pool.wait_ge(x_in[s], (use(s, i) + 1) * 16)
                    pool.wait_ge(stored[s], (i + 1) * 16)
                    pool.tensor_tensor(xres[s][:, :, :], xin[s][:, :, :], wide("bo0"), ALU.add).then_inc(res_made[s], 1)
                    pool.wait_ge(res_made[s], FIRST + i * (LAYERS + 1) + 1)
                    pool.wait_ge(turned[s], 2 * i * LAYERS + 1)
                    pool.sem_inc(x_used[s], 1)
                    return
                pool.wait_ge(normed[s], i * LAYERS + l)
                pool.tensor_tensor(xres[s][:, :, :], y[s][:, :, :], wide(f"g{l - 1}"), ALU.mult).then_inc(scaled[s], 1)
                pool.wait_ge(scaled[s], i * LAYERS + l)
                pool.tensor_tensor(xres[s][:, :, :], xres[s][:, :, :], wide(f"b{l - 1}"), ALU.add).then_inc(res_made[s], 1)

            def values(s, i, l):
                if l != 1:
                    return
                u = use(s, i)
                pool.wait_ge(rest_made[s], u + 1)
                rest = v_rest[s][:, :, :].rearrange("p c (h d) -> p c h d", h=HEADS)
                factor = one[:, 0:1].unsqueeze(2).to_broadcast([P, HEADS, HD])
                for c in range(C):
                    a = pool.tensor_tensor(v_parts[s][:, c, :, 1, 0:HD], rest[:, c], factor, ALU.mult)
                a.then_inc(vc_made[s], 1)
                pool.wait_ge(vc_made[s], 2 * u + 1)
                for c in range(C):
                    a = pool.tensor_tensor(v_parts[s][:, c, :, 0, 0:HD], rest[:, c], v_parts[s][:, c, :, 1, 0:HD],
                                           ALU.subtract)
                a.then_inc(vc_made[s], 1)

            def head_exp_t(s, i, r):
                u = use(s, i)
                pool.wait_ge(head_exp[s], u * HEADS + r + 1)
                if r >= 2:
                    pool.wait_ge(head_done[s], u * HEADS + r - 1)
                pool.tensor_tensor(ht_lo[s][:, r % 2], ht[s][r % 2][:, :, :], ht_hi[s][:, r % 2],
                                   ALU.subtract).then_inc(head_lo[s], 1)

            def mean(s, i, l):
                n = i * LAYERS + l + 1
                pool.wait_ge(mean_made[s], 2 * n)
                pool.tensor_tensor(rstd[s][:, :], var_eps[s][:, :], half[:, :], ALU.pow).then_inc(rstd_made[s], 1)

            all_turns(pool, turns, {"values": values, "residual": residual, "head_exp": head_exp_t,
                                    "mean": mean})


def kernel(x, adj, L0_gnn_Wq, L0_gnn_Wk, L0_gnn_Wv, L0_gnn_Wo, L0_gnn_bo, L0_gnn_gamma, L0_gnn_beta,
           L1_gnn_Wq, L1_gnn_bq, L1_gnn_Wk, L1_gnn_bk, L1_gnn_Wv, L1_gnn_bv, L1_gnn_Wo, L1_gnn_bo, L1_gnn_gamma,
           L1_gnn_beta, L2_gnn_Wq, L2_gnn_bq, L2_gnn_Wk, L2_gnn_bk, L2_gnn_Wc, L2_gnn_ln_g, L2_gnn_ln_b,
           L3_gnn_Wq, L3_gnn_Wk, L3_gnn_Wv, L3_gnn_Wo, L3_gnn_bo, L3_gnn_gamma, L3_gnn_beta):
    import numpy as np
    import concourse.bacc as bacc
    from concourse import mybir as mb
    from concourse.bass_utils import run_bass_kernel_spmd

    a = np.asarray
    qk2 = [np.concatenate([a(L2_gnn_Wq)[k].T, a(L2_gnn_Wk)[k].T], axis=1) for k in range(2)]
    weights = np.stack([a(L0_gnn_Wq).T, a(L0_gnn_Wk).T, a(L0_gnn_Wv).T, a(L0_gnn_Wo),
                        a(L3_gnn_Wq).T, a(L3_gnn_Wk).T, a(L3_gnn_Wv).T, a(L3_gnn_Wo),
                        a(L1_gnn_Wq), a(L1_gnn_Wk), a(L1_gnn_Wv), qk2[0], qk2[1],
                        a(L2_gnn_Wc)[0].T, a(L2_gnn_Wc)[1].T, a(L1_gnn_Wo)])
    g = [a(L0_gnn_gamma), a(L1_gnn_gamma), a(L2_gnn_ln_g)[0], a(L2_gnn_ln_g)[1], a(L3_gnn_gamma)]
    b = [a(L0_gnn_beta), a(L1_gnn_beta), a(L2_gnn_ln_b)[0], a(L2_gnn_ln_b)[1], a(L3_gnn_beta)]
    rows = np.stack(g + b + [a(L0_gnn_bo), a(L1_gnn_bo), a(L3_gnn_bo)])
    rows = np.ascontiguousarray(np.broadcast_to(rows, (128,) + rows.shape))
    bqk2 = [np.concatenate([a(L2_gnn_bq)[k], a(L2_gnn_bk)[k]]) for k in range(2)]
    cols = np.stack(g[:4] + b[:4] + [a(L1_gnn_bq), a(L1_gnn_bk), a(L1_gnn_bv)] + bqk2)
    cols = cols.reshape(len(cols), 2, 128).transpose(2, 0, 1)
    given = {"x": a(x), "adj": a(adj), "weights": weights, "rows": rows, "cols": cols}

    nc = bacc.Bacc("TRN2", target_bir_lowering=False, num_devices=1)
    arrays, args = {}, []
    for name, v in given.items():
        arrays[f"in_{name}"] = v = np.ascontiguousarray(v)
        args.append(nc.dram_tensor(f"in_{name}", v.shape, mb.dt.from_np(v.dtype), kind="ExternalInput").ap())
    args.append(nc.dram_tensor("out_0", given["x"].shape, mb.dt.float32, kind="ExternalOutput").ap())
    graph_stack_kernel(nc, *args)
    return run_bass_kernel_spmd(nc, [arrays], core_ids=[0]).results[0]["out_0"]
```
